# Optimizing a Trainium2 kernel written in Bass

```python
import numpy as np
import jax
import jax.numpy as jnp

def _softmax(x, axis=-1):
    return jax.nn.softmax(x, axis=axis)

def _gelu(x):
    return jax.nn.gelu(x, approximate=True)

def _silu(x):
    return jax.nn.silu(x)

def _sigmoid(x):
    return jax.nn.sigmoid(x)

def _layernorm(x, axis=-1, eps=1e-05):
    m = jnp.mean(x, axis=axis, keepdims=True)
    v = jnp.var(x, axis=axis, keepdims=True)
    return (x - m) / jnp.sqrt(v + eps)

def _scatter_add(tgt, idx, src, axis=0):
    return tgt.at[idx].add(src)

def _segment_sum(src, seg, n):
    return jax.ops.segment_sum(src, seg, n)
kernel_name = 'mk_seq_preln_d2_jaxref_r8_d2143d'

def setup_inputs(seed: int=0):
    np.random.seed(seed)
    _w = jnp.asarray

    def _L0_attn_setup():
        import jax, jax.numpy as jnp
        import numpy as np
        DIM = 128
        HEADS = 16
        DIM_HEAD = DIM // HEADS
        LATENT = DIM // 4
        SCALE = DIM_HEAD ** (-0.5)
        key = jax.random.key(seed)
        ks = jax.random.split(key, 8)
        B, S = (2, 256)
        init = lambda k, shape, fan_in: jax.random.normal(k, shape, jnp.float32) * fan_in ** (-0.5)
        return {'x': jax.random.normal(ks[0], (B, S, DIM), jnp.float32), 'Wq': init(ks[1], (DIM, DIM), DIM), 'bq': jnp.zeros((DIM,), jnp.float32), 'Wl': init(ks[2], (DIM, LATENT), DIM), 'bl': jnp.zeros((LATENT,), jnp.float32), 'Wk': init(ks[3], (LATENT, DIM), LATENT), 'bk': jnp.zeros((DIM,), jnp.float32), 'Wv': init(ks[4], (LATENT, DIM), LATENT), 'bv': jnp.zeros((DIM,), jnp.float32), 'Wo': init(ks[5], (DIM, DIM), DIM), 'bo': jnp.zeros((DIM,), jnp.float32)}
    _L0_attn_in = _L0_attn_setup()

    def _L0_ffn_setup():
        import jax, jax.numpy as jnp
        import numpy as np
        DIM = 128
        DEPTH = 6
        HEADS = 16
        DIM_HEAD = 64
        WINDOW = 32
        INNER = HEADS * DIM_HEAD
        DIM_INNER = int(DIM * 4 * 2 / 3)
        QK_SCALE = 8.0

        def shift_tokens(t):
            a, s = jnp.split(t, 2, -1)
            s = jnp.pad(s, ((0, 0), (1, 0), (0, 0)))[:, :-1]
            return jnp.concatenate([a, s], -1)

        def l2norm(t):
            return t / jnp.maximum(jnp.linalg.norm(t, axis=-1, keepdims=True), 1e-12)

        def rotate_half(x):
            x1, x2 = jnp.split(x, 2, -1)
            return jnp.concatenate([-x2, x1], -1)

        def rotary_tables(n):
            half = jnp.arange(0, DIM_HEAD, 2, dtype=jnp.float32)
            inv_freq = 1.0 / 10000.0 ** (half / DIM_HEAD)
            t = jnp.arange(n, dtype=jnp.float32)
            freqs = t[:, None] * inv_freq[None, :]
            freqs = jnp.concatenate([freqs, freqs], -1)
            base_scale = (half + 0.4 * DIM_HEAD) / (1.4 * DIM_HEAD)
            power = (t - n // 2) / (WINDOW // 2)
            scale = base_scale[None, :] ** power[:, None]
            scale = jnp.concatenate([scale, scale], -1)
            return (freqs, scale)

        def local_attention(q, k, v):
            b, h, n, d = q.shape
            w = WINDOW
            nw = n // w
            bq = q.reshape(b, h, nw, w, d)
            bk = k.reshape(b, h, nw, w, d)
            bv = v.reshape(b, h, nw, w, d)

            def look(t):
                p = jnp.pad(t, ((0, 0), (0, 0), (1, 0), (0, 0), (0, 0)))
                return jnp.concatenate([p[:, :, :nw], p[:, :, 1:]], axis=3)
            bk2, bv2 = (look(bk), look(bv))
            seq = jnp.arange(n).reshape(nw, w)
            seq_p = jnp.pad(seq, ((1, 0), (0, 0)), constant_values=-1)
            jt = jnp.concatenate([seq_p[:nw], seq_p[1:]], axis=1)
            it = seq[:, :, None]
            jb = jt[:, None, :]
            mask = (it < jb) | (it > jb + w) | (jb == -1)
            sim = jnp.einsum('bhwie,bhwje->bhwij', bq, bk2) * QK_SCALE
            sim = jnp.where(mask, -jnp.finfo(sim.dtype).max, sim)
            attn = jax.nn.softmax(sim, -1)
            out = jnp.einsum('bhwij,bhwje->bhwie', attn, bv2)
            return out.reshape(b, h, n, d)

        def attn_layer(x, Wqkv, qs, ksc, Wo):
            b, n, _ = x.shape
            qkv = x @ Wqkv
            q, k, v = jnp.split(qkv, 3, -1)
            sh = lambda t: t.reshape(b, n, HEADS, DIM_HEAD).transpose(0, 2, 1, 3)
            q, k, v = (sh(q), sh(k), sh(v))
            q = l2norm(q) * qs
            k = l2norm(k) * ksc
            freqs, scale = rotary_tables(n)
            cos, sin = (jnp.cos(freqs), jnp.sin(freqs))
            q = q * cos * scale + rotate_half(q) * sin * scale
            inv = 1.0 / scale
            k = k * cos * inv + rotate_half(k) * sin * inv
            out = local_attention(q, k, v)
            out = out.transpose(0, 2, 1, 3).reshape(b, n, INNER)
            return out @ Wo

        def ffn_layer(x, g, bln, W1, b1, W2, b2):
            mu = x.mean(-1, keepdims=True)
            var = ((x - mu) ** 2).mean(-1, keepdims=True)
            xn = (x - mu) / jnp.sqrt(var + 1e-05) * g + bln
            hg = xn @ W1 + b1
            a, gate = jnp.split(hg, 2, -1)
            return a * jax.nn.gelu(gate, approximate=False) @ W2 + b2
        key = jax.random.key(seed)
        ks = jax.random.split(key, 8)
        B, N = (2, 256)
        init = lambda k, shape: jax.random.normal(k, shape, jnp.float32) * 0.02
        return {'x': jax.random.normal(ks[0], (B, N, DIM), jnp.float32), 'Wqkv': init(ks[1], (DEPTH, DIM, 3 * INNER)), 'q_scale': jnp.ones((DEPTH, DIM_HEAD), jnp.float32), 'k_scale': jnp.ones((DEPTH, DIM_HEAD), jnp.float32), 'Wo': init(ks[2], (DEPTH, INNER, DIM)), 'ln_g': jnp.ones((DEPTH, DIM), jnp.float32), 'ln_b': jnp.zeros((DEPTH, DIM), jnp.float32), 'W1': init(ks[3], (DEPTH, DIM, 2 * DIM_INNER)), 'b1': jnp.zeros((DEPTH, 2 * DIM_INNER), jnp.float32), 'W2': init(ks[4], (DEPTH, DIM_INNER, DIM)), 'b2': jnp.zeros((DEPTH, DIM), jnp.float32)}
    _L0_ffn_in = _L0_ffn_setup()

    def _L1_attn_setup():
        import jax, jax.numpy as jnp
        import numpy as np
        D_MODEL, D_STATE, D_CONV, EXPAND, HEADDIM, NGROUPS, CHUNK = (128, 64, 4, 2, 64, 1, 64)
        D_INNER = EXPAND * D_MODEL
        NHEADS = D_INNER // HEADDIM
        CONV_DIM = D_INNER + 2 * NGROUPS * D_STATE
        D_IN_PROJ = 2 * D_INNER + 2 * NGROUPS * D_STATE + NHEADS
        EPS = 1e-05

        def segsum(x):
            T = x.shape[-1]
            i = jnp.arange(T)[:, None]
            j = jnp.arange(T)[None, :]
            xr = jnp.where(i > j, x[..., :, None], 0.0)
            s = jnp.cumsum(xr, axis=-2)
            return jnp.where(i >= j, s, -jnp.inf)

        def _forward(u, in_proj_w, conv_w, conv_b, init_states, dt_bias, A_log, D, norm_w, out_proj_w):
            b, L, _ = u.shape
            zxbcdt = jnp.einsum('bld,ed->ble', u, in_proj_w)
            z = zxbcdt[..., :D_INNER]
            xBC = zxbcdt[..., D_INNER:D_INNER + CONV_DIM]
            dt = jax.nn.softplus(zxbcdt[..., D_INNER + CONV_DIM:] + dt_bias)
            xp = jnp.pad(xBC, ((0, 0), (D_CONV - 1, 0), (0, 0)))
            xBC = sum((xp[:, k:k + L, :] * conv_w[:, k] for k in range(D_CONV))) + conv_b
            xBC = jax.nn.silu(xBC)
            x = xBC[..., :D_INNER].reshape(b, L, NHEADS, HEADDIM)
            Bm = xBC[..., D_INNER:D_INNER + NGROUPS * D_STATE].reshape(b, L, NGROUPS, D_STATE)
            Cm = xBC[..., D_INNER + NGROUPS * D_STATE:].reshape(b, L, NGROUPS, D_STATE)
            A = -jnp.exp(A_log)
            Bm = jnp.repeat(Bm, NHEADS // NGROUPS, axis=2)
            Cm = jnp.repeat(Cm, NHEADS // NGROUPS, axis=2)
            X = x * dt[..., None]
            Adt = A * dt
            c = L // CHUNK
            Xc = X.reshape(b, c, CHUNK, NHEADS, HEADDIM)
            Bc = Bm.reshape(b, c, CHUNK, NHEADS, D_STATE)
            Cc = Cm.reshape(b, c, CHUNK, NHEADS, D_STATE)
            Ac = Adt.reshape(b, c, CHUNK, NHEADS).transpose(0, 3, 1, 2)
            A_cumsum = jnp.cumsum(Ac, axis=-1)
            Lmat = jnp.exp(segsum(Ac))
            Y_diag = jnp.einsum('bclhn,bcshn,bhcls,bcshp->bclhp', Cc, Bc, Lmat, Xc)
            decay_states = jnp.exp(A_cumsum[..., -1:] - A_cumsum)
            states = jnp.einsum('bclhn,bhcl,bclhp->bchpn', Bc, decay_states, Xc)
            init = jnp.broadcast_to(init_states, (b,) + init_states.shape)[:, None]
            states = jnp.concatenate([init, states], axis=1)
            decay_chunk = jnp.exp(segsum(jnp.pad(A_cumsum[..., -1], ((0, 0), (0, 0), (1, 0)))))
            new_states = jnp.einsum('bhzc,bchpn->bzhpn', decay_chunk, states)
            states = new_states[:, :-1]
            state_decay_out = jnp.exp(A_cumsum)
            Y_off = jnp.einsum('bclhn,bchpn,bhcl->bclhp', Cc, states, state_decay_out)
            Y = (Y_diag + Y_off).reshape(b, L, NHEADS, HEADDIM) + x * D[:, None]
            y = Y.reshape(b, L, D_INNER)
            y = y * jax.nn.silu(z)
            y = y * jax.lax.rsqrt(jnp.mean(y * y, axis=-1, keepdims=True) + EPS) * norm_w
            return jnp.einsum('bld,ed->ble', y, out_proj_w)
        key = jax.random.key(seed)
        ks = jax.random.split(key, 10)
        B, L = (4, 512)
        u = jax.random.normal(ks[0], (B, L, D_MODEL), dtype=jnp.float32)
        in_proj_w = jax.random.normal(ks[1], (D_IN_PROJ, D_MODEL), dtype=jnp.float32) * D_MODEL ** (-0.5)
        conv_w = jax.random.normal(ks[2], (CONV_DIM, D_CONV), dtype=jnp.float32) * D_CONV ** (-0.5)
        conv_b = jax.random.normal(ks[3], (CONV_DIM,), dtype=jnp.float32) * 0.02
        init_states = jax.random.normal(ks[4], (NHEADS, HEADDIM, D_STATE), dtype=jnp.float32) * 0.02
        dt = jnp.exp(jax.random.uniform(ks[5], (NHEADS,)) * (np.log(0.1) - np.log(0.001)) + np.log(0.001))
        dt = jnp.clip(dt, 0.0001, None)
        dt_bias = dt + jnp.log(-jnp.expm1(-dt))
        A_log = jnp.log(jax.random.uniform(ks[6], (NHEADS,), minval=1.0, maxval=16.0))
        D = jnp.ones((NHEADS,), dtype=jnp.float32)
        norm_w = jnp.ones((D_INNER,), dtype=jnp.float32)
        out_proj_w = jax.random.normal(ks[7], (D_MODEL, D_INNER), dtype=jnp.float32) * D_INNER ** (-0.5)
        return {'u': u, 'in_proj_w': in_proj_w, 'conv_w': conv_w, 'conv_b': conv_b, 'init_states': init_states, 'dt_bias': dt_bias, 'A_log': A_log, 'D': D, 'norm_w': norm_w, 'out_proj_w': out_proj_w}
    _L1_attn_in = _L1_attn_setup()

    def _L1_ffn_setup():
        import jax, jax.numpy as jnp
        import numpy as np
        DIM = 128
        DEPTH = 2
        HEADS = 8
        DIM_HEAD = 64
        WINDOW = 64
        INNER = HEADS * DIM_HEAD
        HID = int(DIM * 4 * 2 / 3)
        B, N = (2, 1024)
        QK_SCALE = 8.0

        def shift_token(t):
            t1, t2 = jnp.split(t, 2, axis=-1)
            t2 = jnp.pad(t2, ((0, 0), (1, 0), (0, 0)))[:, :-1]
            return jnp.concatenate([t1, t2], axis=-1)

        def l2norm(t):
            return t / jnp.clip(jnp.linalg.norm(t, axis=-1, keepdims=True), 1e-12)

        def rotate_half(x):
            x1, x2 = jnp.split(x, 2, axis=-1)
            return jnp.concatenate([-x2, x1], axis=-1)

        def rotary_xpos(q, k):
            n = q.shape[-2]
            half_idx = jnp.arange(0, DIM_HEAD, 2, dtype=jnp.float32)
            inv_freq = 1.0 / 10000.0 ** (half_idx / DIM_HEAD)
            t = jnp.arange(n, dtype=jnp.float32)
            freqs = t[:, None] * inv_freq[None, :]
            freqs = jnp.concatenate([freqs, freqs], axis=-1)
            base = (half_idx + 0.4 * DIM_HEAD) / (1.4 * DIM_HEAD)
            power = (t - n // 2) / float(WINDOW // 2)
            scale = base[None, :] ** power[:, None]
            scale = jnp.concatenate([scale, scale], axis=-1)
            cos, sin = (jnp.cos(freqs), jnp.sin(freqs))
            q = q * cos * scale + rotate_half(q) * sin * scale
            k = k * cos / scale + rotate_half(k) * sin / scale
            return (q, k)

        def local_attention(q, k, v):
            b, h, n, d = q.shape
            w = n // WINDOW
            bq = q.reshape(b, h, w, WINDOW, d) * QK_SCALE
            bk = k.reshape(b, h, w, WINDOW, d)
            bv = v.reshape(b, h, w, WINDOW, d)

            def look_around(t):
                p = jnp.pad(t, ((0, 0), (0, 0), (1, 0), (0, 0), (0, 0)))
                return jnp.concatenate([p[:, :, :w], p[:, :, 1:]], axis=3)
            bk, bv = (look_around(bk), look_around(bv))
            bt = jnp.arange(n).reshape(w, WINDOW)
            btp = jnp.pad(bt, ((1, 0), (0, 0)), constant_values=-1)
            btk = jnp.concatenate([btp[:w], btp[1:]], axis=1)
            sim = jnp.einsum('bhwid,bhwjd->bhwij', bq, bk)
            i = bt[:, :, None]
            j = btk[:, None, :]
            mask = (i < j) | (i > j + WINDOW) | (j == -1)
            sim = jnp.where(mask, -jnp.finfo(sim.dtype).max, sim)
            attn = jax.nn.softmax(sim, axis=-1)
            out = jnp.einsum('bhwij,bhwjd->bhwid', attn, bv)
            return out.reshape(b, h, n, d)

        def _layer(x, wqkv, qs, ksc, wo, lg, lb, w1, b1, w2, b2):
            b, n, _ = x.shape
            h = shift_token(x)
            qkv = h @ wqkv
            q, k, v = jnp.split(qkv, 3, axis=-1)
            to_heads = lambda t: t.reshape(b, n, HEADS, DIM_HEAD).transpose(0, 2, 1, 3)
            q, k, v = (to_heads(q), to_heads(k), to_heads(v))
            q = l2norm(q) * qs
            k = l2norm(k) * ksc
            q, k = rotary_xpos(q, k)
            o = local_attention(q, k, v)
            o = o.transpose(0, 2, 1, 3).reshape(b, n, INNER)
            x = x + o @ wo
            h = shift_token(x)
            mu = h.mean(-1, keepdims=True)
            var = h.var(-1, keepdims=True)
            h = (h - mu) / jnp.sqrt(var + 1e-05) * lg + lb
            h = h @ w1 + b1
            a, g = jnp.split(h, 2, axis=-1)
            h = a * jax.nn.gelu(g, approximate=False)
            x = x + h @ w2 + b2
            return x
        key = jax.random.key(seed)
        ks = jax.random.split(key, 6)
        return {'x': jax.random.normal(ks[0], (B, N, DIM), jnp.float32), 'wqkv': jax.random.normal(ks[1], (DEPTH, DIM, 3 * INNER), jnp.float32) * 0.02, 'q_scale': jnp.ones((DEPTH, DIM_HEAD), jnp.float32), 'k_scale': jnp.ones((DEPTH, DIM_HEAD), jnp.float32), 'wo': jax.random.normal(ks[2], (DEPTH, INNER, DIM), jnp.float32) * 0.02, 'ln_g': jnp.ones((DEPTH, DIM), jnp.float32), 'ln_b': jnp.zeros((DEPTH, DIM), jnp.float32), 'w1': jax.random.normal(ks[3], (DEPTH, DIM, 2 * HID), jnp.float32) * 0.02, 'b1': jnp.zeros((DEPTH, 2 * HID), jnp.float32), 'w2': jax.random.normal(ks[4], (DEPTH, HID, DIM), jnp.float32) * 0.02, 'b2': jnp.zeros((DEPTH, DIM), jnp.float32)}
    _L1_ffn_in = _L1_ffn_setup()
    _d = {'L0_attn_x': _L0_attn_in['x'], 'L0_attn_Wq': _L0_attn_in['Wq'], 'L0_attn_bq': _L0_attn_in['bq'], 'L0_attn_Wl': _L0_attn_in['Wl'], 'L0_attn_bl': _L0_attn_in['bl'], 'L0_attn_Wk': _L0_attn_in['Wk'], 'L0_attn_bk': _L0_attn_in['bk'], 'L0_attn_Wv': _L0_attn_in['Wv'], 'L0_attn_bv': _L0_attn_in['bv'], 'L0_attn_Wo': _L0_attn_in['Wo'], 'L0_attn_bo': _L0_attn_in['bo'], 'L0_ffn_Wqkv': _L0_ffn_in['Wqkv'], 'L0_ffn_q_scale': _L0_ffn_in['q_scale'], 'L0_ffn_k_scale': _L0_ffn_in['k_scale'], 'L0_ffn_Wo': _L0_ffn_in['Wo'], 'L0_ffn_ln_g': _L0_ffn_in['ln_g'], 'L0_ffn_ln_b': _L0_ffn_in['ln_b'], 'L0_ffn_W1': _L0_ffn_in['W1'], 'L0_ffn_b1': _L0_ffn_in['b1'], 'L0_ffn_W2': _L0_ffn_in['W2'], 'L0_ffn_b2': _L0_ffn_in['b2'], 'L1_attn_in_proj_w': _L1_attn_in['in_proj_w'], 'L1_attn_conv_w': _L1_attn_in['conv_w'], 'L1_attn_conv_b': _L1_attn_in['conv_b'], 'L1_attn_init_states': _L1_attn_in['init_states'], 'L1_attn_dt_bias': _L1_attn_in['dt_bias'], 'L1_attn_A_log': _L1_attn_in['A_log'], 'L1_attn_D': _L1_attn_in['D'], 'L1_attn_norm_w': _L1_attn_in['norm_w'], 'L1_attn_out_proj_w': _L1_attn_in['out_proj_w'], 'L1_ffn_wqkv': _L1_ffn_in['wqkv'], 'L1_ffn_q_scale': _L1_ffn_in['q_scale'], 'L1_ffn_k_scale': _L1_ffn_in['k_scale'], 'L1_ffn_wo': _L1_ffn_in['wo'], 'L1_ffn_ln_g': _L1_ffn_in['ln_g'], 'L1_ffn_ln_b': _L1_ffn_in['ln_b'], 'L1_ffn_w1': _L1_ffn_in['w1'], 'L1_ffn_b1': _L1_ffn_in['b1'], 'L1_ffn_w2': _L1_ffn_in['w2'], 'L1_ffn_b2': _L1_ffn_in['b2']}
    _x0 = _d['L0_attn_x']
    _d['L0_attn_x'] = jax.random.normal(jax.random.fold_in(jax.random.key(seed), 1), (16, 256, 128), dtype=_x0.dtype)
    del _x0
    return _d

def reference(L0_attn_x, L0_attn_Wq, L0_attn_bq, L0_attn_Wl, L0_attn_bl, L0_attn_Wk, L0_attn_bk, L0_attn_Wv, L0_attn_bv, L0_attn_Wo, L0_attn_bo, L0_ffn_Wqkv, L0_ffn_q_scale, L0_ffn_k_scale, L0_ffn_Wo, L0_ffn_ln_g, L0_ffn_ln_b, L0_ffn_W1, L0_ffn_b1, L0_ffn_W2, L0_ffn_b2, L1_attn_in_proj_w, L1_attn_conv_w, L1_attn_conv_b, L1_attn_init_states, L1_attn_dt_bias, L1_attn_A_log, L1_attn_D, L1_attn_norm_w, L1_attn_out_proj_w, L1_ffn_wqkv, L1_ffn_q_scale, L1_ffn_k_scale, L1_ffn_wo, L1_ffn_ln_g, L1_ffn_ln_b, L1_ffn_w1, L1_ffn_b1, L1_ffn_w2, L1_ffn_b2):

    def _L0_attn_ref(x, Wq, bq, Wl, bl, Wk, bk, Wv, bv, Wo, bo):
        import jax, jax.numpy as jnp
        import numpy as np
        DIM = 128
        HEADS = 16
        DIM_HEAD = DIM // HEADS
        LATENT = DIM // 4
        SCALE = DIM_HEAD ** (-0.5)
        B, S, D = x.shape
        H, Dh = (HEADS, DIM_HEAD)
        q = (x @ Wq + bq).reshape(B, S, H, Dh)
        latent = x @ Wl + bl
        k = (latent @ Wk + bk).reshape(B, S, H, Dh)
        v = (latent @ Wv + bv).reshape(B, S, H, Dh)
        scores = jnp.einsum('bihd,bjhd->bhij', q, k) * SCALE
        attn = jax.nn.softmax(scores, axis=-1)
        out = jnp.einsum('bhij,bjhd->bihd', attn, v).reshape(B, S, D)
        out = out @ Wo + bo
        return out

    def _L0_ffn_ref(x, Wqkv, q_scale, k_scale, Wo, ln_g, ln_b, W1, b1, W2, b2):
        import jax, jax.numpy as jnp
        import numpy as np
        DIM = 128
        DEPTH = 6
        HEADS = 16
        DIM_HEAD = 64
        WINDOW = 32
        INNER = HEADS * DIM_HEAD
        DIM_INNER = int(DIM * 4 * 2 / 3)
        QK_SCALE = 8.0

        def shift_tokens(t):
            a, s = jnp.split(t, 2, -1)
            s = jnp.pad(s, ((0, 0), (1, 0), (0, 0)))[:, :-1]
            return jnp.concatenate([a, s], -1)

        def l2norm(t):
            return t / jnp.maximum(jnp.linalg.norm(t, axis=-1, keepdims=True), 1e-12)

        def rotate_half(x):
            x1, x2 = jnp.split(x, 2, -1)
            return jnp.concatenate([-x2, x1], -1)

        def rotary_tables(n):
            half = jnp.arange(0, DIM_HEAD, 2, dtype=jnp.float32)
            inv_freq = 1.0 / 10000.0 ** (half / DIM_HEAD)
            t = jnp.arange(n, dtype=jnp.float32)
            freqs = t[:, None] * inv_freq[None, :]
            freqs = jnp.concatenate([freqs, freqs], -1)
            base_scale = (half + 0.4 * DIM_HEAD) / (1.4 * DIM_HEAD)
            power = (t - n // 2) / (WINDOW // 2)
            scale = base_scale[None, :] ** power[:, None]
            scale = jnp.concatenate([scale, scale], -1)
            return (freqs, scale)

        def local_attention(q, k, v):
            b, h, n, d = q.shape
            w = WINDOW
            nw = n // w
            bq = q.reshape(b, h, nw, w, d)
            bk = k.reshape(b, h, nw, w, d)
            bv = v.reshape(b, h, nw, w, d)

            def look(t):
                p = jnp.pad(t, ((0, 0), (0, 0), (1, 0), (0, 0), (0, 0)))
                return jnp.concatenate([p[:, :, :nw], p[:, :, 1:]], axis=3)
            bk2, bv2 = (look(bk), look(bv))
            seq = jnp.arange(n).reshape(nw, w)
            seq_p = jnp.pad(seq, ((1, 0), (0, 0)), constant_values=-1)
            jt = jnp.concatenate([seq_p[:nw], seq_p[1:]], axis=1)
            it = seq[:, :, None]
            jb = jt[:, None, :]
            mask = (it < jb) | (it > jb + w) | (jb == -1)
            sim = jnp.einsum('bhwie,bhwje->bhwij', bq, bk2) * QK_SCALE
            sim = jnp.where(mask, -jnp.finfo(sim.dtype).max, sim)
            attn = jax.nn.softmax(sim, -1)
            out = jnp.einsum('bhwij,bhwje->bhwie', attn, bv2)
            return out.reshape(b, h, n, d)

        def attn_layer(x, Wqkv, qs, ksc, Wo):
            b, n, _ = x.shape
            qkv = x @ Wqkv
            q, k, v = jnp.split(qkv, 3, -1)
            sh = lambda t: t.reshape(b, n, HEADS, DIM_HEAD).transpose(0, 2, 1, 3)
            q, k, v = (sh(q), sh(k), sh(v))
            q = l2norm(q) * qs
            k = l2norm(k) * ksc
            freqs, scale = rotary_tables(n)
            cos, sin = (jnp.cos(freqs), jnp.sin(freqs))
            q = q * cos * scale + rotate_half(q) * sin * scale
            inv = 1.0 / scale
            k = k * cos * inv + rotate_half(k) * sin * inv
            out = local_attention(q, k, v)
            out = out.transpose(0, 2, 1, 3).reshape(b, n, INNER)
            return out @ Wo

        def ffn_layer(x, g, bln, W1, b1, W2, b2):
            mu = x.mean(-1, keepdims=True)
            var = ((x - mu) ** 2).mean(-1, keepdims=True)
            xn = (x - mu) / jnp.sqrt(var + 1e-05) * g + bln
            hg = xn @ W1 + b1
            a, gate = jnp.split(hg, 2, -1)
            return a * jax.nn.gelu(gate, approximate=False) @ W2 + b2
        for i in range(DEPTH):
            x = attn_layer(shift_tokens(x), Wqkv[i], q_scale[i], k_scale[i], Wo[i]) + x
            x = ffn_layer(shift_tokens(x), ln_g[i], ln_b[i], W1[i], b1[i], W2[i], b2[i]) + x
        return x

    def _L1_attn_ref(u, in_proj_w, conv_w, conv_b, init_states, dt_bias, A_log, D, norm_w, out_proj_w):
        import jax, jax.numpy as jnp
        import numpy as np
        D_MODEL, D_STATE, D_CONV, EXPAND, HEADDIM, NGROUPS, CHUNK = (128, 64, 4, 2, 64, 1, 64)
        D_INNER = EXPAND * D_MODEL
        NHEADS = D_INNER // HEADDIM
        CONV_DIM = D_INNER + 2 * NGROUPS * D_STATE
        D_IN_PROJ = 2 * D_INNER + 2 * NGROUPS * D_STATE + NHEADS
        EPS = 1e-05

        def segsum(x):
            T = x.shape[-1]
            i = jnp.arange(T)[:, None]
            j = jnp.arange(T)[None, :]
            xr = jnp.where(i > j, x[..., :, None], 0.0)
            s = jnp.cumsum(xr, axis=-2)
            return jnp.where(i >= j, s, -jnp.inf)

        def _forward(u, in_proj_w, conv_w, conv_b, init_states, dt_bias, A_log, D, norm_w, out_proj_w):
            b, L, _ = u.shape
            zxbcdt = jnp.einsum('bld,ed->ble', u, in_proj_w)
            z = zxbcdt[..., :D_INNER]
            xBC = zxbcdt[..., D_INNER:D_INNER + CONV_DIM]
            dt = jax.nn.softplus(zxbcdt[..., D_INNER + CONV_DIM:] + dt_bias)
            xp = jnp.pad(xBC, ((0, 0), (D_CONV - 1, 0), (0, 0)))
            xBC = sum((xp[:, k:k + L, :] * conv_w[:, k] for k in range(D_CONV))) + conv_b
            xBC = jax.nn.silu(xBC)
            x = xBC[..., :D_INNER].reshape(b, L, NHEADS, HEADDIM)
            Bm = xBC[..., D_INNER:D_INNER + NGROUPS * D_STATE].reshape(b, L, NGROUPS, D_STATE)
            Cm = xBC[..., D_INNER + NGROUPS * D_STATE:].reshape(b, L, NGROUPS, D_STATE)
            A = -jnp.exp(A_log)
            Bm = jnp.repeat(Bm, NHEADS // NGROUPS, axis=2)
            Cm = jnp.repeat(Cm, NHEADS // NGROUPS, axis=2)
            X = x * dt[..., None]
            Adt = A * dt
            c = L // CHUNK
            Xc = X.reshape(b, c, CHUNK, NHEADS, HEADDIM)
            Bc = Bm.reshape(b, c, CHUNK, NHEADS, D_STATE)
            Cc = Cm.reshape(b, c, CHUNK, NHEADS, D_STATE)
            Ac = Adt.reshape(b, c, CHUNK, NHEADS).transpose(0, 3, 1, 2)
            A_cumsum = jnp.cumsum(Ac, axis=-1)
            Lmat = jnp.exp(segsum(Ac))
            Y_diag = jnp.einsum('bclhn,bcshn,bhcls,bcshp->bclhp', Cc, Bc, Lmat, Xc)
            decay_states = jnp.exp(A_cumsum[..., -1:] - A_cumsum)
            states = jnp.einsum('bclhn,bhcl,bclhp->bchpn', Bc, decay_states, Xc)
            init = jnp.broadcast_to(init_states, (b,) + init_states.shape)[:, None]
            states = jnp.concatenate([init, states], axis=1)
            decay_chunk = jnp.exp(segsum(jnp.pad(A_cumsum[..., -1], ((0, 0), (0, 0), (1, 0)))))
            new_states = jnp.einsum('bhzc,bchpn->bzhpn', decay_chunk, states)
            states = new_states[:, :-1]
            state_decay_out = jnp.exp(A_cumsum)
            Y_off = jnp.einsum('bclhn,bchpn,bhcl->bclhp', Cc, states, state_decay_out)
            Y = (Y_diag + Y_off).reshape(b, L, NHEADS, HEADDIM) + x * D[:, None]
            y = Y.reshape(b, L, D_INNER)
            y = y * jax.nn.silu(z)
            y = y * jax.lax.rsqrt(jnp.mean(y * y, axis=-1, keepdims=True) + EPS) * norm_w
            return jnp.einsum('bld,ed->ble', y, out_proj_w)
        return _forward(u, in_proj_w, conv_w, conv_b, init_states, dt_bias, A_log, D, norm_w, out_proj_w)

    def _L1_ffn_ref(x, wqkv, q_scale, k_scale, wo, ln_g, ln_b, w1, b1, w2, b2):
        import jax, jax.numpy as jnp
        import numpy as np
        DIM = 128
        DEPTH = 2
        HEADS = 8
        DIM_HEAD = 64
        WINDOW = 64
        INNER = HEADS * DIM_HEAD
        HID = int(DIM * 4 * 2 / 3)
        B, N = (2, 1024)
        QK_SCALE = 8.0

        def shift_token(t):
            t1, t2 = jnp.split(t, 2, axis=-1)
            t2 = jnp.pad(t2, ((0, 0), (1, 0), (0, 0)))[:, :-1]
            return jnp.concatenate([t1, t2], axis=-1)

        def l2norm(t):
            return t / jnp.clip(jnp.linalg.norm(t, axis=-1, keepdims=True), 1e-12)

        def rotate_half(x):
            x1, x2 = jnp.split(x, 2, axis=-1)
            return jnp.concatenate([-x2, x1], axis=-1)

        def rotary_xpos(q, k):
            n = q.shape[-2]
            half_idx = jnp.arange(0, DIM_HEAD, 2, dtype=jnp.float32)
            inv_freq = 1.0 / 10000.0 ** (half_idx / DIM_HEAD)
            t = jnp.arange(n, dtype=jnp.float32)
            freqs = t[:, None] * inv_freq[None, :]
            freqs = jnp.concatenate([freqs, freqs], axis=-1)
            base = (half_idx + 0.4 * DIM_HEAD) / (1.4 * DIM_HEAD)
            power = (t - n // 2) / float(WINDOW // 2)
            scale = base[None, :] ** power[:, None]
            scale = jnp.concatenate([scale, scale], axis=-1)
            cos, sin = (jnp.cos(freqs), jnp.sin(freqs))
            q = q * cos * scale + rotate_half(q) * sin * scale
            k = k * cos / scale + rotate_half(k) * sin / scale
            return (q, k)

        def local_attention(q, k, v):
            b, h, n, d = q.shape
            w = n // WINDOW
            bq = q.reshape(b, h, w, WINDOW, d) * QK_SCALE
            bk = k.reshape(b, h, w, WINDOW, d)
            bv = v.reshape(b, h, w, WINDOW, d)

            def look_around(t):
                p = jnp.pad(t, ((0, 0), (0, 0), (1, 0), (0, 0), (0, 0)))
                return jnp.concatenate([p[:, :, :w], p[:, :, 1:]], axis=3)
            bk, bv = (look_around(bk), look_around(bv))
            bt = jnp.arange(n).reshape(w, WINDOW)
            btp = jnp.pad(bt, ((1, 0), (0, 0)), constant_values=-1)
            btk = jnp.concatenate([btp[:w], btp[1:]], axis=1)
            sim = jnp.einsum('bhwid,bhwjd->bhwij', bq, bk)
            i = bt[:, :, None]
            j = btk[:, None, :]
            mask = (i < j) | (i > j + WINDOW) | (j == -1)
            sim = jnp.where(mask, -jnp.finfo(sim.dtype).max, sim)
            attn = jax.nn.softmax(sim, axis=-1)
            out = jnp.einsum('bhwij,bhwjd->bhwid', attn, bv)
            return out.reshape(b, h, n, d)

        def _layer(x, wqkv, qs, ksc, wo, lg, lb, w1, b1, w2, b2):
            b, n, _ = x.shape
            h = shift_token(x)
            qkv = h @ wqkv
            q, k, v = jnp.split(qkv, 3, axis=-1)
            to_heads = lambda t: t.reshape(b, n, HEADS, DIM_HEAD).transpose(0, 2, 1, 3)
            q, k, v = (to_heads(q), to_heads(k), to_heads(v))
            q = l2norm(q) * qs
            k = l2norm(k) * ksc
            q, k = rotary_xpos(q, k)
            o = local_attention(q, k, v)
            o = o.transpose(0, 2, 1, 3).reshape(b, n, INNER)
            x = x + o @ wo
            h = shift_token(x)
            mu = h.mean(-1, keepdims=True)
            var = h.var(-1, keepdims=True)
            h = (h - mu) / jnp.sqrt(var + 1e-05) * lg + lb
            h = h @ w1 + b1
            a, g = jnp.split(h, 2, axis=-1)
            h = a * jax.nn.gelu(g, approximate=False)
            x = x + h @ w2 + b2
            return x
        for l in range(DEPTH):
            x = _layer(x, wqkv[l], q_scale[l], k_scale[l], wo[l], ln_g[l], ln_b[l], w1[l], b1[l], w2[l], b2[l])
        return x
    x = L0_attn_x
    x = x + _L0_attn_ref(_layernorm(x, axis=-1), L0_attn_Wq, L0_attn_bq, L0_attn_Wl, L0_attn_bl, L0_attn_Wk, L0_attn_bk, L0_attn_Wv, L0_attn_bv, L0_attn_Wo, L0_attn_bo)
    x = x + _L0_ffn_ref(_layernorm(x, axis=-1), L0_ffn_Wqkv, L0_ffn_q_scale, L0_ffn_k_scale, L0_ffn_Wo, L0_ffn_ln_g, L0_ffn_ln_b, L0_ffn_W1, L0_ffn_b1, L0_ffn_W2, L0_ffn_b2)
    x = x + _L1_attn_ref(_layernorm(x, axis=-1), L1_attn_in_proj_w, L1_attn_conv_w, L1_attn_conv_b, L1_attn_init_states, L1_attn_dt_bias, L1_attn_A_log, L1_attn_D, L1_attn_norm_w, L1_attn_out_proj_w)
    x = x + _L1_ffn_ref(_layernorm(x, axis=-1), L1_ffn_wqkv, L1_ffn_q_scale, L1_ffn_k_scale, L1_ffn_wo, L1_ffn_ln_g, L1_ffn_ln_b, L1_ffn_w1, L1_ffn_b1, L1_ffn_w2, L1_ffn_b2)
    return x

_drawn_inputs = setup_inputs


def setup_inputs(seed=0):
    import zlib

    import numpy as np

    out = dict(_drawn_inputs(seed))
    spreads = {'L0_attn_bq': (0.0, 0.416),
     'L0_attn_bl': (0.0, 0.1),
     'L0_attn_bk': (0.0, 2.0),
     'L0_attn_bv': (0.0, 0.1),
     'L0_attn_bo': (0.0, 0.1),
     'L0_ffn_q_scale': (1.0, 0.6),
     'L0_ffn_k_scale': (1.0, 0.6),
     'L0_ffn_ln_g': (1.0, 0.6),
     'L0_ffn_ln_b': (0.0, 0.8),
     'L0_ffn_b1': (0.0, 0.8),
     'L0_ffn_b2': (0.0, 0.1),
     'L1_attn_D': (1.0, 0.2),
     'L1_attn_norm_w': (1.0, 0.2),
     'L1_ffn_q_scale': (1.0, 0.6),
     'L1_ffn_k_scale': (1.0, 0.6),
     'L1_ffn_ln_g': (1.0, 0.6),
     'L1_ffn_ln_b': (0.0, 0.8),
     'L1_ffn_b1': (0.0, 0.8),
     'L1_ffn_b2': (0.0, 0.8)}
    factors = {'L0_ffn_W1': 3.262,
     'L0_ffn_W2': 3.218,
     'L1_attn_conv_b': 5.545,
     'L1_attn_init_states': 8.0,
     'L1_ffn_wqkv': 4.155,
     'L1_ffn_wo': 4.206,
     'L1_ffn_w1': 8.0,
     'L1_ffn_w2': 8.0}
    for name, (base, spread) in spreads.items():
        noise = np.random.default_rng([zlib.crc32(name.encode()), seed]).standard_normal(out[name].shape)
        drawn = base * np.exp(spread * noise) if base else spread * noise
        out[name] = jnp.asarray(drawn.astype(out[name].dtype))
    for name, factor in factors.items():
        out[name] = (out[name] * factor).astype(out[name].dtype)
    return out
```

```python
from contextlib import ExitStack

import concourse.bass as bass
from concourse import mybir

ALU = mybir.AluOpType
ACT = mybir.ActivationFunctionType
F32 = mybir.dt.float32
BF16 = mybir.dt.bfloat16
I32 = mybir.dt.int32
AX_X = mybir.AxisListType.X

P = 128
NCH = 8
B, S = 2, 256
T = B * S // P
HD = 64
PAD = 64
BLK = 64
HID = 341
NF = 3
FS = [P, P, HID - 2 * P]
CHUNK = 512
GH = 4
RSQRT_SEED = 1597463007.0
A_HEADS, A_HD, LATENT = 16, 8, 32
M_HEADS, M_INNER, M_STATE, M_TAPS = 4, 256, 64, 4
M_Z, M_X, M_B, M_C, M_DT = 0, 256, 512, 576, 640


def known(v, k):
    return isinstance(v, int) and v == k


def below(v, k):
    return isinstance(v, int) and v < k


class Stage:

    def __init__(self, sem, a, tag, heads, window, layers, pre):
        self.H, self.W, self.LAYERS = heads, window, layers
        self.NK = window + BLK
        self.NQ = heads * HD // CHUNK
        self.J = 4 * self.NQ
        self.G = heads // GH
        self.NO = max(1, heads // 8)
        self.N = layers * NCH
        self.QK = 2 * self.NQ
        self.jobs = [[2], [3], [4, 5], [6, 7]] if self.NQ == 2 else [[2], [3]]
        self.AT_INV = 2 if self.NQ == 2 else 0
        at = ((2, 3, 4, 6, 8, 9, 10, 21, 22), (13, 14, 19)) if self.NQ == 2 else ((1, 2, 2, 3, 4, 5, 5, 13, 14), (7, 9, 10))
        self.AT_WO, self.AT_X1, self.AT_SHIFT, self.AT_TURN, self.AT_NORM, self.AT_BACK, self.AT_XN, self.AT_W2, self.AT_XI = at[0]
        self.AT_FF = at[1]
        self.wqkv, self.wo, self.w1, self.w2 = a[pre + "wqkv"], a[pre + "wo"], a[pre + "w1"], a[pre + "w2"]
        self.vec, self.rows, self.rot, self.mask = a[tag + "_vec"], a[tag + "_rows"], a[tag + "_rot"], a[tag + "_mask"]
        self.w_qkv = sem(f"{tag}_w_qkv")
        self.w_o = sem(f"{tag}_w_o")
        self.w_1 = sem(f"{tag}_w_1")
        self.w_2 = sem(f"{tag}_w_2")
        self.w_vec = sem(f"{tag}_w_vec")
        self.w_rows = sem(f"{tag}_w_rows")
        self.tables = sem(f"{tag}_tables")
        self.h_top = sem(f"{tag}_h_top")
        self.h_top2 = sem(f"{tag}_h_top2")
        self.h_bot2 = sem(f"{tag}_h_bot2")
        self.h_bot = sem(f"{tag}_h_bot")
        self.xi_ready = sem(f"{tag}_xi_ready")
        self.x1_ready = sem(f"{tag}_x1_ready")
        self.proj_full = sem(f"{tag}_proj_full")
        self.sq_ready = sem(f"{tag}_sq_ready")
        self.sum_ready = sem(f"{tag}_sum_ready")
        self.rotated = sem(f"{tag}_rotated")
        self.inv_ready = sem(f"{tag}_inv_ready")
        self.roped = sem(f"{tag}_roped")
        self.qk_turned = sem(f"{tag}_qk_turned")
        self.qk_stored = sem(f"{tag}_qk_stored")
        self.v_stored = sem(f"{tag}_v_stored")
        self.s_full = sem(f"{tag}_s_full")
        self.s_less_max = sem(f"{tag}_s_less_max")
        self.p_ready = sem(f"{tag}_p_ready")
        self.p_turned = sem(f"{tag}_p_turned")
        self.pT_stored = sem(f"{tag}_pT_stored")
        self.o_full = sem(f"{tag}_o_full")
        self.o_ready = sem(f"{tag}_o_ready")
        self.o_turned = sem(f"{tag}_o_turned")
        self.oT_stored = sem(f"{tag}_oT_stored")
        self.wo_full = sem(f"{tag}_wo_full")
        self.ln_turned = sem(f"{tag}_ln_turned")
        self.ln_ready = sem(f"{tag}_ln_ready")
        self.ln_back = sem(f"{tag}_ln_back")
        self.xn_stored = sem(f"{tag}_xn_stored")
        self.a_full = sem(f"{tag}_a_full")
        self.g_full = sem(f"{tag}_g_full")
        self.gelu_ready = sem(f"{tag}_gelu_ready")
        self.hid_ready = sem(f"{tag}_hid_ready")
        self.w2_full = sem(f"{tag}_w2_full")


class Signals:

    def __init__(self, sem):
        self.c_in = sem("s_c_in")
        self.x_in = sem("s_x_in")
        self.a_in = sem("s_a_in")
        self.m_in = sem("s_m_in")
        self.lb_c = sem("s_lb_c")
        self.ld_c = sem("s_ld_c")
        self.zeroed = sem("s_zeroed")
        self.identb_ready = sem("s_identb_ready")
        self.ones_set = sem("s_ones_set")
        self.e_turned = sem("s_e_turned")
        self.e_ready = sem("s_e_ready")
        self.e_back = sem("s_e_back")
        self.e_out = sem("s_e_out")
        self.a_q_full = sem("s_a_q_full")
        self.a_l_full = sem("s_a_l_full")
        self.a_k_full = sem("s_a_k_full")
        self.a_v_full = sem("s_a_v_full")
        self.a_q_st = sem("s_a_q_st")
        self.a_l_st = sem("s_a_l_st")
        self.a_k_st = sem("s_a_k_st")
        self.a_v_st = sem("s_a_v_st")
        self.a_qm_st = sem("s_a_qm_st")
        self.a_s_full = sem("s_a_s_full")
        self.a_less = sem("s_a_less")
        self.a_p = sem("s_a_p")
        self.a_pt = sem("s_a_pt")
        self.a_pT_st = sem("s_a_pT_st")
        self.a_o_full = sem("s_a_o_full")
        self.a_o = sem("s_a_o")
        self.a_ot = sem("s_a_ot")
        self.a_oT_st = sem("s_a_oT_st")
        self.a_acc = sem("s_a_acc")
        self.x_ready = sem("s_x_ready")
        self.m_proj = sem("s_m_proj")
        self.m_cin_st = sem("s_m_cin_st")
        self.m_conv = sem("s_m_conv")
        self.m_xc_st = sem("s_m_xc_st")
        self.m_zfull = sem("s_m_zfull")
        self.m_z_st = sem("s_m_z_st")
        self.m_dtf = sem("s_m_dtf")
        self.m_nv_st = sem("s_m_nv_st")
        self.m_ln = sem("s_m_ln")
        self.m_a_st = sem("s_m_a_st")
        self.m_am_st = sem("s_m_am_st")
        self.m_cumf = sem("s_m_cumf")
        self.m_ecum_st = sem("s_m_ecum_st")
        self.m_cbf = sem("s_m_cbf")
        self.m_cb_st = sem("s_m_cb_st")
        self.m_df = sem("s_m_df")
        self.m_L_st = sem("s_m_L_st")
        self.m_M_st = sem("s_m_M_st")
        self.m_xf = sem("s_m_xf")
        self.m_xdt_st = sem("s_m_xdt_st")
        self.m_yf = sem("s_m_yf")
        self.m_offf = sem("s_m_offf")
        self.m_g = sem("s_m_g")
        self.m_ssr = sem("s_m_ssr")
        self.m_yn = sem("s_m_yn")
        self.m_yt = sem("s_m_yt")
        self.m_yT_st = sem("s_m_yT_st")
        self.m_acc = sem("s_m_acc")
        self.fin_x = sem("s_fin_x")
        self.fin_t = sem("s_fin_t")
        self.fin_st = sem("s_fin_st")
        self.m_x = sem("s_m_x")
        self.m_zeroed = sem("s_m_zeroed")
        self.xT_ready = sem("s_xT_ready")
        self.out_done = sem("s_out_done")
        self.dve_step = sem("s_dve_step")
        self.act_step = sem("s_act_step")
        self.pool_step = sem("s_pool_step")


class Chain:

    def __init__(self, eng, sem):
        self.eng, self.sem, self.base, self.n = eng, sem, 0, 0

    def __call__(self, ins):
        self.n += 1
        ins.then_inc(self.sem, 1)
        self.eng.wait_ge(self.sem, self.base + self.n)

    def enter(self, done, per):
        self.before = self.n
        self.base, self.n, self.per = self.before + done * per, 0, per

    def leave(self, rounds):
        assert self.n == self.per, (self.n, self.per)
        self.base, self.n = 0, self.before + rounds * self.per


def build(nc, a, out):
    ctx = ExitStack()
    with ctx:
        def sb(name, shape, dt=F32):
            return ctx.enter_context(nc.sbuf_tensor(name, shape, dt))

        def sem(name):
            return ctx.enter_context(nc.semaphore(name))

        BS = B * S

        ident = sb("ident", [P, P])
        identb = sb("identb", [P, P], BF16)
        upper = sb("upper", [P, 3 * P])
        strict = sb("strict", [P, P])
        headmask = sb("headmask", [P, A_HEADS])

        x_all = sb("x_all", [P, NCH * B * S])
        xi_all = sb("xi_all", [P, NCH * B * S])
        xT = sb("xT", [P, B * S])
        x1 = sb("x1", [P, B * S])
        hT = sb("hT", [P, B, PAD + S])
        fT = sb("fT", [P, B, 1 + S])
        xnT = sb("xnT", [P, B * S])
        xin = sb("xin", [P, T, P])
        ln_h = sb("ln_h", [P, T, P])
        ln_st = sb("ln_st", [P, T, 6])
        ln_mv = sb("ln_mv", [P, 6, T])
        nw_y = sb("nw_y", [P, 32])
        nw_t = sb("nw_t", [P, 32 + T])
        nw_s = sb("nw_s", [P, 32 + T])

        proj = [ctx.enter_context(nc.psum_tensor(f"proj{i}", [P, CHUNK], F32)) for i in range(2)]
        turn = [ctx.enter_context(nc.psum_tensor(f"turn{i}", [P, CHUNK], F32)) for i in range(2)]
        sc = [ctx.enter_context(nc.psum_tensor(f"sc{i}", [P, CHUNK], F32)) for i in range(2)]
        ops = ctx.enter_context(nc.psum_tensor("ops", [P, CHUNK], F32))
        acc = ctx.enter_context(nc.psum_tensor("acc", [P, CHUNK], F32))

        NP_ = 4
        prob = [sb(f"prob{i}", [P, CHUNK]) for i in range(NP_)]
        probT = [sb(f"probT{i}", [P, CHUNK]) for i in range(2)]
        nmax = [sb(f"nmax{i}", [P, GH]) for i in range(2)]
        rden = [sb(f"rden{i}", [P, A_HEADS]) for i in range(2)]
        o_tok = [sb(f"o_tok{i}", [P, 16 * HD]) for i in range(2)]
        oT = sb("oT", [P, 8, B * S])

        A = {k: a["L0_attn_" + k] for k in ("Wq", "Wl", "Wk", "Wv", "Wo")}
        a_wq, a_wo = sb("a_wq", [P, P]), sb("a_wo", [P, P])
        a_wl = sb("a_wl", [P, LATENT])
        a_wk, a_wv = sb("a_wk", [LATENT, P]), sb("a_wv", [LATENT, P])
        a_b = sb("a_b", [P, 4])
        a_bv = sb("a_bv", [P, P])
        rcs = sb("rcs", [P, 8 * CHUNK])
        a_q, a_k, a_lat = rcs[:, 0:B * S], rcs[:, B * S:2 * B * S], rcs[0:LATENT, 2 * B * S:3 * B * S]
        region = sb("region", [P, A_HEADS * B * S])

        def part(lo, shape):
            n = 1
            for d in shape:
                n *= d
            v = region[:, lo:lo + n]
            dims = " ".join(f"d{i}" for i in range(len(shape)))
            return v.rearrange(f"p ({dims}) -> p {dims}", **{f"d{i}": d for i, d in enumerate(shape)})
        a_qm = part(0, [A_HEADS, B * S])
        a_v = rcs[:, 3 * BS:3 * BS + T * A_HEADS * (A_HD + 1)].rearrange("p (t h d) -> p t h d", t=T, h=A_HEADS)

        lb = Stage(sem, a, "lb", 16, 32, 6, "L0f_")
        ld = Stage(sem, a, "ld", 8, 64, 2, "L1f_")
        wqkv = sb("wqkv", [P, 3 * 16 * HD])
        wo = sb("wo", [P, 8, P])
        w1 = sb("w1", [P, 2 * HID])
        w2 = sb("w2", [P, NF, P])
        vec = sb("vec", [P, 9])
        rows = sb("rows", [P, 4 * HD])
        rot = sb("rot", [P, 2, 4 * HD])
        rots = sb("rots", [P, 2, 4 * HD])
        maskf = sb("maskf", [P, 2, BLK + 64])
        mask = sb("mask", [P, 2, CHUNK], BF16)
        sq = [part((15 - i) * BS, [CHUNK]) for i in range(2)]
        rc = [rcs[:, i * CHUNK:(i + 1) * CHUNK] for i in range(4)]
        rs = [rcs[:, (4 + i) * CHUNK:(5 + i) * CHUNK] for i in range(4)]
        ssq = sb("ssq", [P, 32])
        inv = [sb(f"inv{i}", [P, 32 + T]) for i in range(2)]
        qT = part(0, [8, BS])
        kT = sb("kT", [P, 8, B, PAD + S])
        vb = [sb(f"vb{i}", [P, 2, 16, HD + 1]) for i in range(2)]
        gg = [part((8 + i) * BS, [BS]) for i in range(2)]
        hid = part(10 * BS, [NF, BS])

        m_win = sb("m_win", [P, M_DT + M_HEADS])
        m_wout = sb("m_wout", [P, 2, P])
        m_cw = sb("m_cw", [P, 4, M_TAPS + 1])
        m_nw = sb("m_nw", [P, 2])
        m_rows = sb("m_rows", [P, 3, M_HEADS])
        m_init = sb("m_init", [M_STATE, M_HEADS, HD])
        XP = M_TAPS - 1
        o_flat = oT[:].rearrange("p c t -> p (c t)")
        NCIN = 4 * B * (XP + S)
        m_cin = o_flat[:, 0:NCIN].rearrange("p (j b t) -> p j b t", j=4, b=B)
        m_cv = part(0, [4, BS])
        m_xc = part(4 * BS, [4, BS])
        m_z = rcs[:, 6 * BS:8 * BS].rearrange("p (t n) -> p t n", t=T)
        m_v = sb("m_v", [P, T * M_HEADS])
        m_nv = sb("m_nv", [P, T * M_HEADS])
        m_r = sb("m_r", [P, T * M_HEADS])
        m_e = sb("m_e", [P, T * M_HEADS])
        m_dt = sb("m_dt", [P, T * M_HEADS])
        m_eA = sb("m_eA", [P, M_HEADS])
        m_a = sb("m_a", [P, T * M_HEADS])
        m_ecum = sb("m_ecum", [P, T * M_HEADS])
        m_am = rcs[:, 0:4 * BS].rearrange("p (n k) -> p n k", k=P)
        m_ab = rcs[:, 4 * BS:6 * BS].rearrange("p (n k) -> p n k", k=P)
        m_cb = o_flat[:, NCIN:NCIN + B * 3 * P].rearrange("p (b k) -> p b k", b=B)
        m_L = [o_flat[:, NCIN + (B + i) * 3 * P:NCIN + (B + i + 1) * 3 * P] for i in range(2)]
        m_M = [prob[i][:, 0:3 * P] for i in range(2)]
        m_xdt = part(8 * BS, [T, M_INNER])
        m_y = part(10 * BS, [T, M_INNER])
        m_off = part(12 * BS, [T, M_INNER])
        m_ss = sb("m_ss", [P, T])
        m_yT = part(14 * BS, [2, BS])
        out_sb = xin

        s = Signals(sem)

        block = ctx.enter_context(nc.Block())

        def tile_of(t):
            return t // 2, slice(PAD + P * (t % 2), PAD + P * (t % 2) + P)

        def xi_of(ch):
            return xi_all[:, bass.ts(ch, B * S)]

        def x_of(ch):
            return x_all[:, bass.ts(ch, B * S)]

        def head_of(g, j):
            return 8 * (g // 2) + 2 * j + g % 2

        @block.sync
        def _(sp):
            x_dram = a["x"].rearrange("(c b) (u p) d -> c p (b u) d", c=NCH, p=P)
            sp.dma_start(xin[:], x_dram[0]).then_inc(s.x_in, 16)
            for dst, src in ((ident, "c_ident"), (upper, "c_upper"), (strict, "c_strict"), (headmask, "c_headmask")):
                sp.dma_start(dst[:], a[src]).then_inc(s.c_in, 16)
            for dst, src in ((a_wl, A["Wl"]), (a_wq, A["Wq"]), (a_wk, A["Wk"]), (a_wv, A["Wv"]), (a_b, a["a_cols"])):
                sp.dma_start(dst[:], src).then_inc(s.a_in, 16)
            sp.dma_start(a_bv[:], a["L0_attn_bv"].rearrange("(o n) -> o n", o=1).to_broadcast([P, P])).then_inc(s.a_in, 16)
            sp.dma_start(a_wo[:], A["Wo"]).then_inc(s.a_in, 16)
            for dst, src in ((m_win, "m_win"), (m_cw, "m_cw"), (m_nw, "m_nw"), (m_init, "m_init")):
                sp.dma_start(dst[:], a[src]).then_inc(s.m_in, 16)
            sp.dma_start(m_wout[:], a["m_wout"].rearrange("(c p) n -> p c n", p=P)).then_inc(s.m_in, 16)
            sp.dma_start(m_rows[:], a["m_rows"].rearrange("(o r) h -> o r h", o=1).to_broadcast([P, 3, M_HEADS])).then_inc(s.m_in, 16)
            with sp.Fori(1, NCH) as ch:
                sp.wait_ge(s.e_turned, 2 * ch - 1)
                sp.wait_ge(s.e_ready, 2 * ch - 1)
                sp.dma_start(xin[:], x_dram[ch]).then_inc(s.x_in, 16)

            def layers(c, consts):
                sp.dma_start(rot[:], c.rot).then_inc(consts, 16)
                sp.dma_start(maskf[:, :, 0:c.NK], c.mask).then_inc(consts, 16)
                inner = c.H * HD

                def load_rows(L):
                    sp.dma_start(rows[:], c.rows[L].rearrange("(o n) -> o n", o=1).to_broadcast([P, 4 * HD])).then_inc(c.w_rows, 16)

                def load_qkv(L):
                    sp.dma_start(wqkv[:, 0:3 * inner], c.wqkv[L]).then_inc(c.w_qkv, 16)

                def load_o(L):
                    sp.dma_start(wo[:, 0:c.H // 2, :], c.wo[L].rearrange("(c p) n -> p c n", p=P)).then_inc(c.w_o, 16)

                def load_ff(L):
                    sp.dma_start(w1[:], c.w1[L]).then_inc(c.w_1, 16)
                    sp.dma_start(w2[:, 0:2, :], c.w2[L, 0:2 * P, :].rearrange("(c p) n -> p c n", p=P)).then_inc(c.w_2, 16)
                    sp.dma_start(w2[0:FS[2], 2, :], c.w2[L, 2 * P:HID, :]).then_inc(c.w_2, 16)

                def load_vec(L):
                    sp.dma_start(vec[:], c.vec[L]).then_inc(c.w_vec, 16)

                for load in (load_rows, load_qkv, load_o, load_ff, load_vec):
                    load(0)
                with sp.Fori(1, c.LAYERS) as L:
                    n = L * NCH
                    sp.wait_ge(c.tables, L)
                    load_rows(L)
                    sp.wait_ge(c.proj_full, n * (T * c.J))
                    load_qkv(L)
                    sp.wait_ge(c.wo_full, n)
                    load_o(L)
                    sp.wait_ge(c.w2_full, n)
                    load_ff(L)
                    sp.wait_ge(c.xi_ready, n)
                    load_vec(L)

            layers(lb, s.lb_c)
            sp.wait_ge(s.m_x, 1)
            layers(ld, s.ld_c)

            o_dram = out.rearrange("(c b) (u p) d -> c p (b u) d", c=NCH, p=P)
            with sp.Fori(0, NCH) as ch:
                sp.wait_ge(s.fin_st, ch + 1)
                sp.dma_start(o_dram[ch], out_sb[:]).then_inc(s.out_done, 16)
            sp.wait_ge(s.out_done, 16 * NCH)

        @block.gpsimd
        def _(pool):
            link = Chain(pool, s.pool_step)
            pool.memset(hT[:], 0.0).then_inc(s.zeroed, 1)
            pool.memset(fT[:], 0.0).then_inc(s.zeroed, 1)
            pool.memset(kT[:, :, :, 0:PAD], 0.0).then_inc(s.zeroed, 1)
            pool.memset(a_v, 1.0).then_inc(s.ones_set, 1)
            for v in vb:
                pool.memset(v[:, :, :, HD:HD + 1], 1.0).then_inc(s.ones_set, 1)

            def tables(c):
                pool.tensor_tensor(rots[:], rot[:], rows[:].rearrange("p (o n) -> p o n", o=1).to_broadcast([P, 2, 4 * HD]),
                                   ALU.mult).then_inc(c.tables, 1)

            def layers(c, consts):
                per = T * 2 * c.NQ
                pool.wait_ge(consts, 32)
                with pool.Fori(0, c.LAYERS) as L:
                    pool.wait_ge(c.w_rows, L * 16 + 16)
                    tables(c)
                    with pool.Fori(0, NCH) as ch:
                        n = L * NCH + ch
                        link.enter(n, per)
                        for t in range(T):
                            for m in range(2 * c.NQ):
                                k = t * 2 * c.NQ + m
                                pool.wait_ge(c.rotated, n * per + k + 1)
                                link(pool.tensor_tensor(rc[k % 4], rc[k % 4], rs[k % 4], ALU.add))
                            pool.wait_ge(c.inv_ready, n * T + t + 1)
                            for m in range(2 * c.NQ):
                                v = rc[(t * 2 * c.NQ + m) % 4].rearrange("p (h d) -> p h d", d=HD)
                                w = inv[t % 2][:, 8 * m:8 * m + 8].rearrange("p (h o) -> p h o", o=1).to_broadcast([P, 8, HD])
                                pool.tensor_tensor(v, v, w, ALU.mult).then_inc(c.roped, 1)
                        link.leave(c.LAYERS * NCH)
            layers(lb, s.lb_c)

            pool.wait_ge(s.c_in, 64)
            pool.wait_ge(s.m_x, 1)
            pool.memset(m_cin[:, :, :, 0:XP], 0.0).then_inc(s.m_zeroed, 1)
            with pool.Fori(0, NCH) as ch:
                pool.wait_ge(s.m_a_st, ch + 1)
                for b in range(B):
                    for h in range(M_HEADS):
                        for u in range(2):
                            i = (2 * b + u) * M_HEADS + h
                            pool.tensor_tensor(m_am[:, i, :], strict[:], m_a[:, i:i + 1].to_broadcast([P, P]), ALU.mult).then_inc(s.m_am_st, 1)
                        pool.tensor_tensor(m_ab[:, b * M_HEADS + h, :], upper[:, 2 * P:3 * P], m_a[:, i:i + 1].to_broadcast([P, P]),
                                           ALU.mult).then_inc(s.m_am_st, 1)
            layers(ld, s.ld_c)

        @block.scalar
        def _(act):
            link = Chain(act, s.act_step)

            def copy(out_, in_):
                return act.activation(out_, in_, ACT.Copy)

            act.wait_ge(s.a_in, 112)
            with act.Fori(0, NCH) as ch:
                act.wait_ge(s.e_back, ch * 2 + 1)
                copy(xnT[:], turn[1][:]).then_inc(s.e_out, 1)
                act.wait_ge(s.a_q_full, ch + 1)
                act.activation(a_q, proj[0][:], ACT.Identity, bias=a_b[:, 0:1]).then_inc(s.a_q_st, 1)
                act.wait_ge(s.a_l_full, ch + 1)
                act.activation(a_lat, proj[1][0:LATENT, :], ACT.Identity, bias=a_b[0:LATENT, 3:4]).then_inc(s.a_l_st, 1)
                act.wait_ge(s.a_k_full, ch + 1)
                act.activation(a_k, sc[0][:], ACT.Identity, bias=a_b[:, 1:2]).then_inc(s.a_k_st, 1)
                AG = A_HEADS // 2

                def a_exp(n):
                    act.wait_ge(s.a_less, ch * 32 + n + 1)
                    act.activation(prob[n % NP_][:], prob[n % NP_][:], ACT.Exp).then_inc(s.a_p, 1)

                def a_pT(n):
                    act.wait_ge(s.a_pt, ch * 32 + n + 1)
                    if n >= 2:
                        act.wait_ge(s.a_o_full, ch * 32 + n - 1)
                    copy(probT[n % 2][:], turn[n % 2][:]).then_inc(s.a_pT_st, 1)

                def a_oT(t):
                    act.wait_ge(s.a_ot, ch * 4 + t + 1)
                    copy(oT[:, 0, t * P:(t + 1) * P], proj[t % 2][:, 0:P]).then_inc(s.a_oT_st, 1)

                for n in range(T * AG + 1):
                    if n < T * AG:
                        a_exp(n)
                    if n >= 1:
                        a_pT(n - 1)
                    if n >= AG + 3 and (n - 3) % AG == 0:
                        a_oT((n - 3) // AG - 1)
                a_oT(T - 1)

            def layers(c, before):
                QK = c.QK

                def shift(n):
                    if not known(n, 0):
                        act.wait_ge(c.proj_full, n * (T * c.J))
                    copy(hT[64:P, :, PAD + 1:PAD + S],
                         xi_of(n % NCH)[64:P, :].rearrange("p (b t) -> p b t", b=B)[:, :, 0:S - 1]).then_inc(c.h_bot, 1)

                def squares(u, t, j):
                    k = t * QK + j
                    act.wait_ge(c.proj_full, u * c.J + j + 1)
                    if not (known(u, 0) and j < 2):
                        act.wait_ge(c.sum_ready, u * QK + j - 1)
                    act.activation(sq[k % 2], proj[j % 2][:], ACT.Square).then_inc(c.sq_ready, 1)

                def v_store(u, t, j, early):
                    act.wait_ge(c.proj_full, u * c.J + QK + j + 1)
                    if not early:
                        act.wait_ge(c.o_full, (u - 1) * c.G)
                    blk, bank = j // c.NQ, j % c.NQ
                    copy(vb[t % 2][0:c.NK, blk, 8 * bank:8 * bank + 8, 0:HD],
                         proj[j % 2][0:c.NK, :].rearrange("p (h d) -> p h d", d=HD)).then_inc(c.v_stored, 1)

                def qk_store(u, t, j):
                    act.wait_ge(c.qk_turned, u * QK + j + 1)
                    bank, b, cols = j // 2, t // 2, tile_of(t)[1]
                    src = turn[j % 2][:].rearrange("p (r t) -> p r t", t=P)
                    dst = kT[:, 4 * bank:4 * bank + 4, b, cols] if j % 2 else qT[:, 4 * bank:4 * bank + 4, t * P:(t + 1) * P]
                    copy(dst, src).then_inc(c.qk_stored, 1)

                def exp(u, t, g):
                    act.wait_ge(c.s_less_max, u * c.G + g + 1)
                    p = prob[(t * c.G + g) % NP_][:, 0:GH * c.NK]
                    act.activation(p, p, ACT.Exp).then_inc(c.p_ready, 1)

                def pT_store(u, t, g):
                    k = t * c.G + g
                    act.wait_ge(c.p_turned, u * c.G + g + 1)
                    if not (known(u, 0) and g < 2):
                        act.wait_ge(c.o_full, u * c.G + g - 1)
                    copy(probT[k % 2][0:c.NK, :], turn[g % 2][0:c.NK, :]).then_inc(c.pT_stored, 1)

                def oT_store(u, t):
                    for i in range(c.NO):
                        act.wait_ge(c.o_turned, u * c.NO + i + 1)
                        copy(oT[:, 4 * i:4 * i + 4, t * P:(t + 1) * P],
                             turn[i % 2][:].rearrange("p (r t) -> p r t", t=P)).then_inc(c.oT_stored, 1)

                def feed_forward(m, at):
                    if at == c.AT_SHIFT:
                        act.wait_ge(c.x1_ready, m + 1)
                        copy(fT[64:P, :, 2:1 + S],
                             x1[64:P, :].rearrange("p (b t) -> p b t", b=B)[:, :, 0:S - 1]).then_inc(c.h_bot2, 1)
                    if at == c.AT_XN:
                        act.wait_ge(c.w_vec, (m // NCH) * 16 + 16)
                        act.wait_ge(c.ln_back, m + 1)
                        act.activation(xnT[:], acc[:], ACT.Identity, bias=vec[:, 1:2], scale=vec[:, 0:1]).then_inc(c.xn_stored, 1)
                    if at in c.AT_FF:
                        i = c.AT_FF.index(at)
                        act.wait_ge(c.g_full, m * NF + i + 1)
                        if i >= 2:
                            act.wait_ge(c.hid_ready, m * NF + i - 1)
                        act.activation(gg[i % 2][0:FS[i], :], turn[at % 2][0:FS[i], :], ACT.Gelu,
                                       bias=vec[0:FS[i], 6 + i:7 + i]).then_inc(c.gelu_ready, 1)

                def body(n, last=False):
                    first = known(n, 0)
                    for t in range(T):
                        u = n * T + t
                        nxt = t + 1 < T or not last
                        for st in range(c.G + 2):
                            at = t * (c.G + 2) + st
                            if nxt and st < c.G:
                                for j in c.jobs[st]:
                                    if j < QK:
                                        squares(u + 1, (t + 1) % T, j)
                                    else:
                                        v_store(u + 1, (t + 1) % T, j - QK, first and t == 0)
                            if st < c.G:
                                exp(u, t, st)
                            if 1 <= st <= c.G:
                                pT_store(u, t, st - 1)
                            if st == 0 and not (first and t == 0):
                                if t == 1 and not first:
                                    act.wait_ge(c.wo_full, n)
                                oT_store(u - 1, (t - 1) % T)
                            if st >= c.G and nxt:
                                for j in range(c.NQ):
                                    qk_store(u + 1, (t + 1) % T, (st - c.G) * c.NQ + j)
                            if t == T - 2 and st == c.G - 1 and not last:
                                shift(n + 1)
                            if st >= c.G and (t + 2 < T or not last):
                                squares(u + 2, (t + 2) % T, st - c.G)
                            if not first:
                                feed_forward(n - 1, at)

                act.wait_ge(s.x_ready, before)
                shift(0)
                for j in range(QK):
                    squares(0, 0, j)
                for j in range(QK):
                    v_store(0, 0, j, True)
                for j in range(QK):
                    qk_store(0, 0, j)
                for j in range(2):
                    squares(1, 1, j)
                body(0)
                with act.Fori(1, c.N - 1) as n:
                    body(n)
                body(c.N - 1, last=True)
                oT_store(c.N * T - 1, T - 1)
                for at in range(c.AT_XI + 1):
                    feed_forward(c.N - 1, at)

            act.wait_ge(s.zeroed, 3)
            act.wait_ge(s.ones_set, 3)
            layers(lb, NCH)

            act.wait_ge(s.m_in, 96)
            act.wait_ge(s.m_zeroed, 1)
            link(act.activation(m_eA[:], m_rows[:, 1, :], ACT.Exp))
            with act.Fori(0, NCH) as ch:
                link.enter(ch, 1)
                act.wait_ge(s.e_back, 2 * NCH + 2 * ch + 1)
                copy(xnT[:], turn[1][:]).then_inc(s.e_out, 1)
                act.wait_ge(s.m_nv_st, ch + 1)
                link(act.activation(m_e[:], m_nv[:], ACT.Exp))
                act.activation(m_e[:], m_e[:], ACT.Ln, bias=1.0).then_inc(s.m_ln, 1)
                for j in range(4):
                    rows_ = P if j < 2 else M_STATE
                    act.wait_ge(s.m_proj, ch * 4 + j + 1)
                    copy(m_cin[0:rows_, j, :, XP:XP + S],
                         (proj[0], proj[1], sc[0], sc[1])[j][0:rows_, :].rearrange("p (b t) -> p b t", b=B)).then_inc(s.m_cin_st, 1)
                for i in range(2):
                    act.wait_ge(s.m_zfull, ch * 2 + i + 1)
                    act.activation(m_z[:, 2 * i:2 * i + 2, :], proj[i][:].rearrange("p (u n) -> p u n", u=2),
                                   ACT.Silu).then_inc(s.m_z_st, 1)
                for j in range(4):
                    rows_ = P if j < 2 else M_STATE
                    act.wait_ge(s.m_conv, ch * 4 + j + 1)
                    act.activation(m_xc[0:rows_, j, :], m_cv[0:rows_, j, :], ACT.Silu,
                                   bias=m_cw[0:rows_, j, M_TAPS:M_TAPS + 1]).then_inc(s.m_xc_st, 1)
                act.wait_ge(s.m_cumf, ch + 1)
                act.activation(m_ecum[:], acc[:, 64:64 + T * M_HEADS], ACT.Exp).then_inc(s.m_ecum_st, 1)
                for n in range(B * M_HEADS):
                    act.wait_ge(s.m_df, ch * 8 + n + 1)
                    if n >= 2:
                        act.wait_ge(s.m_M_st, ch * 8 + n - 1)
                    act.activation(m_L[n % 2], turn[n % 2][:, 0:3 * P], ACT.Exp).then_inc(s.m_L_st, 1)
                for t in range(T):
                    act.wait_ge(s.m_g, ch * 4 + t + 1)
                    act.activation(m_off[:, t, :], m_y[:, t, :], ACT.Square, accum_out=m_ss[:, t:t + 1]).then_inc(s.m_ssr, 1)
                for i in range(2):
                    act.wait_ge(s.m_yt, ch * 2 + i + 1)
                    act.activation(m_yT[:, i, :], turn[i][:], ACT.Copy, scale=m_nw[:, i:i + 1]).then_inc(s.m_yT_st, 1)
                link.leave(NCH)

            layers(ld, 2 * NCH)

            with act.Fori(0, NCH) as ch:
                act.wait_ge(s.fin_t, ch + 1)
                copy(out_sb[:], turn[0][:].rearrange("p (t d) -> p t d", d=P)).then_inc(s.fin_st, 1)
                act.wait_ge(s.out_done, 16 * ch + 16)

        @block.vector
        def _(dve):
            link = Chain(dve, s.dve_step)

            def rsqrt(y, src, tmp):
                yi = y.bitcast(I32)
                link(dve.tensor_scalar(yi, src.bitcast(I32), 1, None, ALU.logical_shift_right))
                link(dve.tensor_scalar(yi, yi, -1.0, RSQRT_SEED, ALU.mult, ALU.add))
                for _ in range(3):
                    link(dve.scalar_tensor_tensor(tmp, y, -0.5, y, ALU.mult, ALU.mult))
                    link(dve.tensor_tensor(tmp, tmp, src, ALU.mult))
                    link(dve.scalar_tensor_tensor(y, tmp, 1.5, y, ALU.add, ALU.mult))
            RSQRT = 11

            def moments(src, var):
                for t in range(T):
                    last = dve.bn_stats(ln_st[:, t, :], src[:, t * P:(t + 1) * P])
                link(last)
                even, odd = ln_st[:, :, 1], ln_st[:, :, 4]
                dve.tensor_tensor(ln_mv[:, 0, :], even, odd, ALU.add)
                dve.tensor_tensor(ln_mv[:, 1, :], even, odd, ALU.subtract)
                link(dve.tensor_tensor(ln_mv[:, 2, :], ln_st[:, :, 2], ln_st[:, :, 5], ALU.add))
                dve.tensor_scalar(ln_mv[:, 3, :], ln_mv[:, 0, :], 0.5, None, ALU.mult)
                dve.scalar_tensor_tensor(ln_mv[:, 4, :], ln_mv[:, 1, :], 0.25, ln_mv[:, 1, :], ALU.mult, ALU.mult)
                link(dve.tensor_scalar(ln_mv[:, 5, :], ln_mv[:, 2, :], 1.0 / P, 1e-5, ALU.mult, ALU.add))
                link(dve.tensor_tensor(var, ln_mv[:, 4, :], ln_mv[:, 5, :], ALU.add))

            def normed(src, factor):
                for t in range(T):
                    last = dve.tensor_scalar(ln_h[:, t, :], src[:, t * P:(t + 1) * P], ln_mv[:, 3, t:t + 1], factor[:, t:t + 1],
                                             ALU.subtract, ALU.mult)
                return last

            def layer_norm(src):
                moments(src, nw_s[:, 0:T])
                rsqrt(nw_y[:, 0:T], nw_s[:, 0:T], nw_t[:, 0:T])
                return normed(src, nw_y)
            LN_STEPS = 4 + RSQRT

            dve.wait_ge(s.c_in, 64)
            dve.tensor_copy(identb[:], ident[:]).then_inc(s.identb_ready, 1)
            def finish(ch, norm):
                dve.sem_inc(s.xT_ready, 1)
                dve.tensor_scalar(x_of(ch), xT[:], 1.0, None, ALU.mult)
                dve.wait_ge(s.e_turned, norm)
                layer_norm(turn[0][:]).then_inc(s.e_ready, 1)
                dve.wait_ge(s.e_back, norm)
                link(dve.tensor_scalar(xi_of(ch), turn[1][:], 1.0, None, ALU.mult))
                dve.sem_inc(s.x_ready, 1)
            FINISH = LN_STEPS + 1

            with dve.Fori(0, NCH) as ch:
                link.enter(ch, LN_STEPS + 1 + T * (A_HEADS // 2) + T + 1 + FINISH)
                dve.wait_ge(s.x_in, ch * 16 + 16)
                layer_norm(xin[:].rearrange("p t d -> p (t d)")).then_inc(s.e_ready, 1)
                dve.wait_ge(s.e_turned, ch * 2 + 1)
                link(dve.tensor_copy(xT[:], turn[0][:]))
                dve.wait_ge(s.a_in, 96)
                dve.wait_ge(s.a_q_st, ch + 1)
                for h in range(A_HEADS):
                    dve.tensor_scalar(a_qm[:, h, :], a_q, headmask[:, h:h + 1], None, ALU.mult).then_inc(s.a_qm_st, 1)
                dve.wait_ge(s.ones_set, 1)
                for t in range(T):
                    dve.wait_ge(s.a_v_full, ch * 4 + t + 1)
                    dve.tensor_tensor(a_v[:, t, :, 0:A_HD],
                                      acc[:, t * P:(t + 1) * P].rearrange("p (h d) -> p h d", d=A_HD),
                                      a_bv[:].rearrange("p (h d) -> p h d", d=A_HD), ALU.add).then_inc(s.a_v_st, 1)
                AG = A_HEADS // 2

                def a_less_max(n):
                    dve.wait_ge(s.a_s_full, ch * 32 + n + 1)
                    v = sc[n % 2][:].rearrange("p (h k) -> p h k", h=2)
                    if n >= 2:
                        dve.wait_ge(s.a_less, ch * 32 + n - 1)
                    link(dve.tensor_reduce(nmax[n % 2][:, 0:2], v, AX_X, ALU.max, negate=True))
                    if n >= NP_:
                        dve.wait_ge(s.a_pt, ch * 32 + n - NP_ + 1)
                    dve.tensor_tensor(prob[n % NP_][:].rearrange("p (h k) -> p h k", h=2), v,
                                      nmax[n % 2][:, 0:2].rearrange("p (h o) -> p h o", o=1).to_broadcast([P, 2, S]),
                                      ALU.add).then_inc(s.a_less, 1)

                def a_norm(t):
                    dve.wait_ge(s.a_o_full, ch * 32 + AG * (t + 1))
                    v = ops[:, 0:A_HEADS * (A_HD + 1)].rearrange("p (h d) -> p h d", d=A_HD + 1)
                    if t >= 2:
                        dve.wait_ge(s.a_o, ch * 4 + t - 1)
                    link(dve.reciprocal(rden[t % 2][:], v[:, :, A_HD]))
                    dve.tensor_tensor(o_tok[t % 2][:, 0:P].rearrange("p (h d) -> p h d", d=A_HD), v[:, :, 0:A_HD],
                                      rden[t % 2][:].rearrange("p (h o) -> p h o", o=1).to_broadcast([P, A_HEADS, A_HD]),
                                      ALU.mult).then_inc(s.a_o, 1)

                for n in range(T * AG):
                    a_less_max(n)
                    if n >= AG + 1 and (n - 1) % AG == 0:
                        a_norm((n - 1) // AG - 1)
                a_norm(T - 1)
                dve.wait_ge(s.a_acc, ch + 1)
                link(dve.scalar_tensor_tensor(xT[:], acc[:], a_b[:, 2:3], xT[:], ALU.add, ALU.add))
                finish(ch, 2 * ch + 2)
                link.leave(NCH)

            def layers(c, consts):
                QK = 2 * c.NQ
                dve.wait_ge(consts, 32)
                for i in range(2):
                    link(dve.tensor_copy(mask[:, i, 0:GH * c.NK].rearrange("p (h k) -> p h k", h=GH),
                                         maskf[:, i:i + 1, 0:c.NK].to_broadcast([P, GH, c.NK])))
                per = T * (1 + RSQRT) + T * c.G * 2 + 4 + NF + 1 + 1

                def shift(n):
                    if not known(n, 0):
                        dve.wait_ge(c.proj_full, n * (T * c.J))
                    dve.tensor_scalar(hT[0:64, :, PAD:PAD + S],
                                      xi_of(n % NCH)[0:64, :].rearrange("p (b t) -> p b t", b=B),
                                      1.0, None, ALU.mult).then_inc(c.h_top, 1)

                def rotate(u, t, j):
                    k = t * QK + j
                    dve.wait_ge(c.sq_ready, u * QK + j + 1)
                    dve.tensor_reduce(ssq[:, 8 * j:8 * j + 8], sq[k % 2].rearrange("p (h d) -> p h d", d=HD),
                                      AX_X, ALU.add).then_inc(c.sum_ready, 1)
                    if not known(u, 0) and (QK == 4 or not known(u, 1)):
                        dve.wait_ge(c.qk_turned, u * QK + j - 3)
                    q = proj[j % 2][:].rearrange("p (h r d) -> p h r d", r=2, d=HD // 2)
                    kind = 2 * HD * (j % 2)
                    tab = [rots[:, t % 2:t % 2 + 1, kind + i * HD:kind + (i + 1) * HD].rearrange("p o (r d) -> p o r d", r=2)
                           .to_broadcast([P, 8, 2, HD // 2]) for i in range(2)]
                    dve.tensor_tensor(rc[k % 4].rearrange("p (h r d) -> p h r d", r=2, d=HD // 2), q, tab[0], ALU.mult)
                    dve.tensor_tensor(rs[k % 4].rearrange("p (h r d) -> p h r d", r=2, d=HD // 2), q[:, :, ::-1, :],
                                      tab[1], ALU.mult).then_inc(c.rotated, 1)

                w = 8 * QK

                def inverse_norms(u, t, early, more):
                    dve.wait_ge(c.sum_ready, (u + 1) * QK)
                    link(dve.tensor_scalar(nw_s[:, 0:w], ssq[:, 0:w], 1e-24, None, ALU.max))
                    if not early:
                        dve.wait_ge(c.roped, (u - 1) * QK)
                    n = w + more
                    rsqrt(inv[t % 2][:, 0:n], nw_s[:, 0:n], nw_t[:, 0:n])
                    dve.sem_inc(c.inv_ready, 1)

                def less_max(u, t, g):
                    k = t * c.G + g
                    v = sc[g % 2][:, 0:GH * c.NK].rearrange("p (h k) -> p h k", h=GH)
                    dve.wait_ge(c.s_full, u * c.G + g + 1)
                    if not (known(u, 0) and g < 2):
                        dve.wait_ge(c.s_less_max, u * c.G + g - 1)
                    link(dve.tensor_reduce(nmax[k % 2][:], v, AX_X, ALU.max, negate=True))
                    if not below(u * c.G + g, NP_):
                        dve.wait_ge(c.p_turned, u * c.G + g - NP_ + 1)
                    dve.tensor_tensor(prob[k % NP_][:, 0:GH * c.NK].rearrange("p (h k) -> p h k", h=GH), v,
                                      nmax[k % 2][:].rearrange("p (h o) -> p h o", o=1).to_broadcast([P, GH, c.NK]),
                                      ALU.add).then_inc(c.s_less_max, 1)

                def normalise(u, t, g, early):
                    k = t * c.G + g
                    v = ops[:, 0:GH * (HD + 1)].rearrange("p (h d) -> p h d", d=HD + 1)
                    dve.wait_ge(c.o_full, u * c.G + g + 1)
                    if not (known(u, 0) and g < 2):
                        dve.wait_ge(c.o_ready, u * c.G + g - 1)
                    link(dve.reciprocal(rden[k % 2][:, 0:GH], v[:, :, HD]))
                    if g == 0 and not early:
                        dve.wait_ge(c.o_turned, (u - 1) * c.NO)
                    dst = o_tok[t % 2][:, 0:c.H * HD].rearrange("p (w j r d) -> p w r j d", j=GH, r=2, d=HD)[:, g // 2, g % 2]
                    dve.tensor_tensor(dst, v[:, :, 0:HD],
                                      rden[k % 2][:, 0:GH].rearrange("p (h o) -> p h o", o=1).to_broadcast([P, GH, HD]),
                                      ALU.mult).then_inc(c.o_ready, 1)

                def means(m):
                    dve.wait_ge(c.ln_turned, m + 1)
                    moments(acc[:], nw_s[:, w:w + T])

                def feed_forward(m, at):
                    if at == c.AT_X1:
                        dve.wait_ge(c.wo_full, m + 1)
                        link(dve.tensor_tensor(x1[:], acc[:], xi_of(m % NCH), ALU.add))
                        dve.sem_inc(c.x1_ready, 1)
                        dve.tensor_scalar(fT[0:64, :, 1:1 + S], x1[0:64, :].rearrange("p (b t) -> p b t", b=B),
                                          1.0, None, ALU.mult).then_inc(c.h_top2, 1)
                    if at == c.AT_NORM:
                        if known(m, c.N - 1):
                            means(m)
                        if known(m, c.N - 1):
                            rsqrt(nw_y[:, 0:T], nw_s[:, w:w + T], nw_t[:, 0:T])
                            factor = nw_y
                        else:
                            factor = inv[(at // (c.G + 2) + 1) % 2][:, w:w + T]
                        normed(acc[:], factor).then_inc(c.ln_ready, 1)
                    if at in c.AT_FF:
                        i = c.AT_FF.index(at)
                        dve.wait_ge(c.w_vec, (m // NCH) * 16 + 16)
                        dve.wait_ge(c.a_full, m * NF + i + 1)
                        dve.wait_ge(c.gelu_ready, m * NF + i + 1)
                        link(dve.scalar_tensor_tensor(hid[0:FS[i], i, :], acc[0:FS[i], :], vec[0:FS[i], 3 + i:4 + i],
                                                      gg[i % 2][0:FS[i], :], ALU.add, ALU.mult))
                        dve.sem_inc(c.hid_ready, 1)
                    if at == c.AT_XI:
                        dve.wait_ge(c.w2_full, m + 1)
                        link(dve.scalar_tensor_tensor(xi_of(m % NCH), acc[:], vec[:, 2:3], x1[:], ALU.add, ALU.add))
                        dve.sem_inc(c.xi_ready, 1)

                def body(n, last=False):
                    first = known(n, 0)
                    for t in range(T):
                        u = n * T + t
                        nxt = t + 1 < T or not last
                        for st in range(c.G + 2):
                            at = t * (c.G + 2) + st
                            if st < c.G:
                                less_max(u, t, st)
                            if nxt and st < c.G:
                                for j in c.jobs[st]:
                                    if j < QK:
                                        rotate(u + 1, (t + 1) % T, j)
                                if at == c.AT_NORM and not first:
                                    means(n - 1)
                                if st == c.AT_INV:
                                    inverse_norms(u + 1, (t + 1) % T, first and t == 0, T if at == c.AT_NORM and not first else 0)
                            if st >= 2:
                                normalise(u, t, st - 2, first and t < 2)
                            if t == T - 2 and st == c.G - 1 and not last:
                                shift(n + 1)
                            if st >= c.G and (t + 2 < T or not last):
                                if t == T - 2 and st == c.G:
                                    dve.wait_ge(c.tables, (n + 1) // NCH + 1)
                                rotate(u + 2, (t + 2) % T, st - c.G)
                            if not first:
                                feed_forward(n - 1, at)

                shift(0)
                dve.wait_ge(c.tables, 1)
                for j in range(QK):
                    rotate(0, 0, j)
                inverse_norms(0, 0, True, 0)
                for j in range(2):
                    rotate(1, 1, j)
                body(0)
                with dve.Fori(1, c.N - 1) as n:
                    link.enter(n - 1, per)
                    body(n)
                    link.leave(c.N - 2)
                body(c.N - 1, last=True)
                for at in range(c.AT_XI + 1):
                    feed_forward(c.N - 1, at)
            layers(lb, s.lb_c)

            dve.wait_ge(s.m_in, 96)
            with dve.Fori(0, NCH) as ch:
                link.enter(ch, 1 + LN_STEPS + 6 + 4 * M_TAPS + 2 + B + 2 * B + 2 * B + 1 + RSQRT + 1 + FINISH)
                link(dve.tensor_tensor(xT[:], x_of(ch), xi_of(ch), ALU.add))
                dve.sem_inc(s.m_x, 1)
                dve.wait_ge(s.e_turned, 2 * NCH + 2 * ch + 1)
                layer_norm(turn[0][:]).then_inc(s.e_ready, 1)

                def bc(v, n):
                    return v.rearrange("p (t h o) -> p t h o", h=M_HEADS, o=1).to_broadcast([P, v.shape[1] // M_HEADS, M_HEADS, n])

                dve.wait_ge(s.m_dtf, ch + 1)
                link(dve.tensor_tensor(m_v[:].rearrange("p (t h) -> p t h", h=M_HEADS),
                                       acc[:, 0:T * M_HEADS].rearrange("p (t h) -> p t h", h=M_HEADS),
                                       m_rows[:, 0:1, :].to_broadcast([P, T, M_HEADS]), ALU.add))
                link(dve.tensor_scalar(m_nv[:], m_v[:], -1.0, None, ALU.mult))
                dve.tensor_tensor(m_nv[:], m_v[:], m_nv[:], ALU.min).then_inc(s.m_nv_st, 1)
                link(dve.tensor_scalar(m_r[:], m_v[:], 0.0, None, ALU.max))
                dve.wait_ge(s.m_ln, ch + 1)
                link(dve.tensor_tensor(m_dt[:], m_r[:], m_e[:], ALU.add))
                link(dve.tensor_tensor(m_a[:].rearrange("p (t h) -> p t h", h=M_HEADS), m_dt[:].rearrange("p (t h) -> p t h", h=M_HEADS),
                                       m_eA[:].rearrange("p (o h) -> p o h", o=1).to_broadcast([P, T, M_HEADS]), ALU.mult))
                link(dve.tensor_scalar(m_a[:], m_a[:], -1.0, None, ALU.mult))
                dve.sem_inc(s.m_a_st, 1)
                for j in range(4):
                    r = P if j < 2 else M_STATE
                    dve.wait_ge(s.m_cin_st, ch * 4 + j + 1)
                    o = m_cv[0:r, j, :].rearrange("p (b t) -> p b t", b=B)
                    link(dve.tensor_scalar(o, m_cin[0:r, j, :, 0:S], m_cw[0:r, j, 0:1], None, ALU.mult))
                    for k in range(1, M_TAPS):
                        link(dve.scalar_tensor_tensor(o, m_cin[0:r, j, :, k:k + S], m_cw[0:r, j, k:k + 1], o, ALU.mult, ALU.add))
                    dve.sem_inc(s.m_conv, 1)
                for i in range(2):
                    dve.wait_ge(s.m_xf, ch * 2 + i + 1)
                    v = sc[i][:].rearrange("p (t h d) -> p t h d", t=2, d=HD)
                    dve.tensor_tensor(m_xdt[:, 2 * i:2 * i + 2, :].rearrange("p t (h d) -> p t h d", d=HD), v,
                                      bc(m_dt[:, 8 * i:8 * i + 8], HD), ALU.mult)
                    link(dve.tensor_tensor(m_y[:, 2 * i:2 * i + 2, :].rearrange("p t (h d) -> p t h d", d=HD), v,
                                           m_rows[:, 2:3, :].rearrange("p o (h u) -> p o h u", u=1).to_broadcast([P, 2, M_HEADS, HD]),
                                           ALU.mult))
                    dve.sem_inc(s.m_xdt_st, 1)
                for b in range(B):
                    dve.wait_ge(s.m_cbf, ch * 2 + b + 1)
                    link(dve.tensor_tensor(m_cb[:, b, :], proj[b][:, 0:3 * P], upper[:], ALU.mult))
                dve.sem_inc(s.m_cb_st, 1)
                dve.wait_ge(s.m_ecum_st, ch + 1)

                def off(b):
                    dve.wait_ge(s.m_offf, ch * 2 + b + 1)
                    link(dve.tensor_tensor(m_off[:, 2 * b:2 * b + 2, :].rearrange("p t (h d) -> p t h d", d=HD),
                                           sc[b][:].rearrange("p (t h d) -> p t h d", t=2, d=HD),
                                           bc(m_ecum[:, 8 * b:8 * b + 8], HD), ALU.mult))
                    y = m_y[:, 2 * b:2 * b + 2, :]
                    link(dve.tensor_tensor(y, y, m_off[:, 2 * b:2 * b + 2, :], ALU.add))
                for n in range(B * M_HEADS):
                    b = n // M_HEADS
                    dve.wait_ge(s.m_L_st, ch * 8 + n + 1)
                    if n >= 2:
                        dve.wait_ge(s.m_yf, ch * 8 + n - 1)
                    dve.tensor_tensor(m_M[n % 2], m_L[n % 2], m_cb[:, b, :], ALU.mult).then_inc(s.m_M_st, 1)
                    if n % M_HEADS == 0:
                        off(b)
                for b in range(B):
                    dve.wait_ge(s.m_yf, ch * 8 + M_HEADS * (b + 1))
                    y = m_y[:, 2 * b:2 * b + 2, :]
                    link(dve.tensor_tensor(y, (ops, acc)[b][:].rearrange("p (t n) -> p t n", t=2), y, ALU.add))
                    dve.wait_ge(s.m_z_st, ch * 2 + b + 1)
                    link(dve.tensor_tensor(y, y, m_z[:, 2 * b:2 * b + 2, :], ALU.mult))
                    dve.sem_inc(s.m_g, 2)
                dve.wait_ge(s.m_ssr, ch * 4 + T)
                link(dve.tensor_scalar(nw_s[:, 0:T], m_ss[:], 1.0 / M_INNER, 1e-5, ALU.mult, ALU.add))
                rsqrt(nw_y[:, 0:T], nw_s[:, 0:T], nw_t[:, 0:T])
                for t in range(T):
                    dve.tensor_scalar(m_y[:, t, :], m_y[:, t, :], nw_y[:, t:t + 1], None, ALU.mult).then_inc(s.m_yn, 1)
                dve.wait_ge(s.m_acc, ch + 1)
                link(dve.tensor_tensor(xT[:], acc[:], xT[:], ALU.add))
                finish(ch, 2 * NCH + 2 * ch + 2)
                link.leave(NCH)

            layers(ld, s.ld_c)
            with dve.Fori(0, NCH) as ch:
                link.enter(ch, 1)
                link(dve.tensor_tensor(xT[:], x_of(ch), xi_of(ch), ALU.add))
                dve.sem_inc(s.fin_x, 1)
                dve.wait_ge(s.fin_t, ch + 1)
                link.leave(NCH)

        @block.tensor
        def _(pe):
            def mm(o, l, r, start=True, stop=True):
                return pe.matmul(o, l, r, start=start, stop=stop, skip_group_check=True)

            def turn_tiles(dst, src):
                for t in range(T):
                    last = pe.transpose(dst[:, t * P:(t + 1) * P], src(t), ident[:])
                return last

            def finish(done):
                pe.wait_ge(s.xT_ready, done)
                turn_tiles(turn[0], lambda t: xT[:, t * P:(t + 1) * P]).then_inc(s.e_turned, 1)
                pe.wait_ge(s.e_ready, 2 * done)
                turn_tiles(turn[1], lambda t: ln_h[:, t, :]).then_inc(s.e_back, 1)

            pe.wait_ge(s.c_in, 64)
            pe.wait_ge(s.a_in, 112)
            with pe.Fori(0, NCH) as ch:
                pe.wait_ge(s.x_in, ch * 16 + 16)
                turn_tiles(turn[0], lambda t: xin[:, t, :]).then_inc(s.e_turned, 1)
                pe.wait_ge(s.e_ready, ch * 2 + 1)
                turn_tiles(turn[1], lambda t: ln_h[:, t, :]).then_inc(s.e_back, 1)
                pe.wait_ge(s.e_out, ch + 1)
                mm(proj[0][:], a_wq[:], xnT[:]).then_inc(s.a_q_full, 1)
                mm(proj[1][0:LATENT, :], a_wl[:], xnT[:]).then_inc(s.a_l_full, 1)
                pe.wait_ge(s.a_l_st, ch + 1)
                mm(sc[0][:], a_wk[:], a_lat).then_inc(s.a_k_full, 1)
                for t in range(T):
                    last = mm(acc[:, t * P:(t + 1) * P], a_lat[:, t * P:(t + 1) * P], a_wv[:])
                last.then_inc(s.a_v_full, T)
                AG = A_HEADS // 2
                pe.wait_ge(s.a_k_st, ch + 1)

                def a_scores(n):
                    t, g = n // AG, n % AG
                    pe.wait_ge(s.a_qm_st, ch * 16 + 2 * g + 2 if t == 0 else A_HEADS)
                    if n >= 2:
                        pe.wait_ge(s.a_less, ch * 32 + n - 1)
                    for i in range(2):
                        last = mm(sc[n % 2][:, i * S:(i + 1) * S], a_qm[:, 2 * g + i, t * P:(t + 1) * P],
                                  a_k[:, (t // 2) * S:(t // 2 + 1) * S])
                    last.then_inc(s.a_s_full, 1)

                def a_turn(n):
                    pe.wait_ge(s.a_p, ch * 32 + n + 1)
                    if n >= 2:
                        pe.wait_ge(s.a_pT_st, ch * 32 + n - 1)
                    for i in range(4):
                        last = pe.transpose(turn[n % 2][:, i * P:(i + 1) * P], prob[n % NP_][:, i * P:(i + 1) * P], ident[:])
                    last.then_inc(s.a_pt, 1)

                def a_values(n):
                    t, g = n // AG, n % AG
                    pe.wait_ge(s.a_pT_st, ch * 32 + n + 1)
                    if n == 0:
                        pe.wait_ge(s.a_v_st, ch * 4 + T)
                    if g == 0 and t >= 1:
                        pe.wait_ge(s.a_o, ch * 4 + t)
                    for i in range(2):
                        h = 2 * g + i
                        for u in range(2):
                            last = mm(ops[:, h * (A_HD + 1):(h + 1) * (A_HD + 1)],
                                      probT[n % 2][:, (2 * i + u) * P:(2 * i + u + 1) * P],
                                      a_v[:, 2 * (t // 2) + u, h, :], start=(u == 0), stop=(u == 1))
                    last.then_inc(s.a_o_full, 1)

                def a_out_turn(t):
                    pe.wait_ge(s.a_o, ch * 4 + t + 1)
                    pe.transpose(proj[t % 2][:, 0:P], o_tok[t % 2][:, 0:P], ident[:]).then_inc(s.a_ot, 1)

                def a_out(t):
                    pe.wait_ge(s.a_oT_st, ch * 4 + t + 1)
                    return mm(acc[:, t * P:(t + 1) * P], a_wo[:], oT[:, 0, t * P:(t + 1) * P])

                for n in range(T * AG + 2):
                    if n < T * AG:
                        a_scores(n)
                    if 1 <= n <= T * AG:
                        a_turn(n - 1)
                    if n >= 2:
                        a_values(n - 2)
                    if n >= AG + 3 and (n - 3) % AG == 0:
                        a_out_turn((n - 3) // AG - 1)
                    if n >= AG + 5 and (n - 5) % AG == 0:
                        a_out((n - 5) // AG - 1)
                a_out_turn(T - 1)
                a_out(T - 1).then_inc(s.a_acc, 1)
                finish(ch + 1)
                pe.wait_ge(s.x_ready, ch + 1)

            def layers(c):
                QK = c.QK
                inner = c.H * HD
                turn_free = [None, None]

                def take_turn(i, sem_, value):
                    if turn_free[i] is not None:
                        pe.wait_ge(*turn_free[i])
                    turn_free[i] = (sem_, value)

                def project(u, t, j):
                    if j >= 2:
                        i = j - 2
                        if i < QK:
                            pe.wait_ge(c.rotated, u * QK + i + 1)
                        else:
                            pe.wait_ge(c.v_stored, u * QK + i - QK + 1)
                    elif not known(u, 0):
                        pe.wait_ge(c.v_stored, u * QK + j - 1)
                    b, cols = tile_of(t)
                    if j < QK:
                        o = (j % 2) * inner + (j // 2) * CHUNK
                        mm(proj[j % 2][:], hT[:, b, cols], wqkv[:, o:o + CHUNK]).then_inc(c.proj_full, 1)
                    else:
                        blk, bank = (j - QK) // c.NQ, (j - QK) % c.NQ
                        first = cols.start + BLK * blk - c.W
                        o = 2 * inner + bank * CHUNK
                        mm(proj[j % 2][0:c.NK, :], hT[:, b, first:first + c.NK], wqkv[:, o:o + CHUNK]).then_inc(c.proj_full, 1)

                def turn_qk(u, t, j):
                    pe.wait_ge(c.roped, u * QK + j + 1)
                    take_turn(j % 2, c.qk_stored, u * QK + j + 1)
                    for i in range(4):
                        last = pe.transpose(turn[j % 2][:, i * P:(i + 1) * P], rc[(t * QK + j) % 4][:, i * P:(i + 1) * P], ident[:])
                    last.then_inc(c.qk_turned, 1)

                def scores(u, t, g):
                    if not (known(u, 0) and g < 2):
                        pe.wait_ge(c.s_less_max, u * c.G + g - 1)
                    if g == 0:
                        pe.wait_ge(c.qk_stored, (u + 1) * QK)
                    mm(sc[g % 2][:, 0:GH * c.NK], identb[:], mask[:, t % 2, 0:GH * c.NK], stop=False)
                    b, cols = tile_of(t)
                    for j in range(GH):
                        h = head_of(g, j)
                        r = slice(HD * (h % 2), HD * (h % 2) + HD)
                        for blk in range(2):
                            first = cols.start + BLK * blk - c.W
                            last = mm(sc[g % 2][BLK * blk:BLK * (blk + 1), j * c.NK:(j + 1) * c.NK],
                                      qT[r, h // 2, t * P + BLK * blk:t * P + BLK * (blk + 1)],
                                      kT[r, h // 2, b, first:first + c.NK], start=False)
                    last.then_inc(c.s_full, 1)

                def turn_p(u, t, g):
                    pe.wait_ge(c.p_ready, u * c.G + g + 1)
                    take_turn(g % 2, c.pT_stored, u * c.G + g + 1)
                    for j in range(GH):
                        last = pe.transpose(turn[g % 2][0:c.NK, j * P:(j + 1) * P],
                                            prob[(t * c.G + g) % NP_][:, j * c.NK:(j + 1) * c.NK], ident[:])
                    last.then_inc(c.p_turned, 1)

                def values(u, t, g):
                    pe.wait_ge(c.pT_stored, u * c.G + g + 1)
                    if g == 0:
                        pe.wait_ge(c.v_stored, (u + 1) * QK)
                    if not (known(u, 0) and g == 0):
                        pe.wait_ge(c.o_ready, u * c.G + g)
                    for j in range(GH):
                        h = head_of(g, j)
                        for blk in range(2):
                            last = mm(ops[BLK * blk:BLK * (blk + 1), j * (HD + 1):(j + 1) * (HD + 1)],
                                      probT[(t * c.G + g) % 2][0:c.NK, j * P + BLK * blk:j * P + BLK * (blk + 1)],
                                      vb[t % 2][0:c.NK, blk, h, :])
                    last.then_inc(c.o_full, 1)

                def turn_o(u, t):
                    pe.wait_ge(c.o_ready, (u + 1) * c.G)
                    for i in range(c.NO):
                        take_turn(i % 2, c.oT_stored, u * c.NO + i + 1)
                        for r in range(4):
                            last = pe.transpose(turn[i % 2][:, r * P:(r + 1) * P],
                                                o_tok[t % 2][:, (4 * i + r) * P:(4 * i + r + 1) * P], ident[:])
                        last.then_inc(c.o_turned, 1)

                def feed_forward(m, at):
                    if at == c.AT_WO:
                        pe.wait_ge(c.oT_stored, (m + 1) * T * c.NO)
                        pe.wait_ge(c.w_o, (m // NCH) * 16 + 16)
                        if not known(m, 0):
                            pe.wait_ge(c.xi_ready, m)
                        for r in range(c.H // 2):
                            last = mm(acc[:], wo[:, r, :], oT[:, r, :], start=(r == 0), stop=(r == c.H // 2 - 1))
                        last.then_inc(c.wo_full, 1)
                    if at == c.AT_TURN:
                        pe.wait_ge(c.h_top2, m + 1)
                        pe.wait_ge(c.h_bot2, m + 1)
                        turn_tiles(acc, lambda t: fT[:, t // 2, 1 + P * (t % 2):1 + P * (t % 2) + P]).then_inc(c.ln_turned, 1)
                    if at == c.AT_BACK:
                        pe.wait_ge(c.ln_ready, m + 1)
                        turn_tiles(acc, lambda t: ln_h[:, t, :]).then_inc(c.ln_back, 1)
                    if at in c.AT_FF:
                        i, bank = c.AT_FF.index(at), at % 2
                        pe.wait_ge(c.w_1, (m // NCH) * 16 + 16)
                        pe.wait_ge(c.xn_stored, m + 1)
                        take_turn(bank, c.gelu_ready, m * NF + i + 1)
                        mm(turn[bank][0:FS[i], :], w1[:, HID + i * P:HID + i * P + FS[i]], xnT[:]).then_inc(c.g_full, 1)
                        if i > 0:
                            pe.wait_ge(c.hid_ready, m * NF + i)
                        mm(acc[0:FS[i], :], w1[:, i * P:i * P + FS[i]], xnT[:]).then_inc(c.a_full, 1)
                    if at == c.AT_W2:
                        pe.wait_ge(c.w_2, (m // NCH) * 32 + 32)
                        pe.wait_ge(c.hid_ready, m * NF + NF)
                        for i in range(NF):
                            last = mm(acc[:], w2[0:FS[i], i, :], hid[0:FS[i], i, :], start=(i == 0), stop=(i == NF - 1))
                        last.then_inc(c.w2_full, 1)

                def body(n, last=False):
                    first = known(n, 0)
                    turn_free[0], turn_free[1] = (c.qk_stored, n * (T * QK) + QK - 1), (c.qk_stored, n * (T * QK) + QK)
                    for t in range(T):
                        u = n * T + t
                        nxt = t + 1 < T or not last
                        for st in range(c.G + 2):
                            at = t * (c.G + 2) + st
                            if st < c.G:
                                scores(u, t, st)
                            if nxt and st < c.G:
                                for j in c.jobs[st]:
                                    project(u + 1, (t + 1) % T, j)
                            if 1 <= st <= c.G:
                                turn_p(u, t, st - 1)
                            if st == 0 and not (first and t == 0):
                                turn_o(u - 1, (t - 1) % T)
                            if st >= 2:
                                values(u, t, st - 2)
                            if st >= c.G and nxt:
                                for j in range(c.NQ):
                                    turn_qk(u + 1, (t + 1) % T, (st - c.G) * c.NQ + j)
                            if st >= c.G and (t + 2 < T or not last):
                                if t == T - 2 and st == c.G:
                                    pe.wait_ge(c.w_qkv, ((n + 1) // NCH) * 16 + 16)
                                    pe.wait_ge(c.h_top, n + 2)
                                    pe.wait_ge(c.h_bot, n + 2)
                                project(u + 2, (t + 2) % T, st - c.G)
                            if not first:
                                feed_forward(n - 1, at)

                pe.wait_ge(c.w_qkv, 16)
                pe.wait_ge(c.h_top, 1)
                pe.wait_ge(c.h_bot, 1)
                for j in range(c.J):
                    project(0, 0, j)
                for j in range(QK):
                    turn_qk(0, 0, j)
                for j in range(2):
                    project(1, 1, j)
                body(0)
                with pe.Fori(1, c.N - 1) as n:
                    body(n)
                body(c.N - 1, last=True)
                turn_o(c.N * T - 1, T - 1)
                for at in range(c.AT_XI + 1):
                    feed_forward(c.N - 1, at)

            pe.wait_ge(s.identb_ready, 1)
            layers(lb)

            pe.wait_ge(s.m_in, 96)
            with pe.Fori(0, NCH) as ch:
                pe.wait_ge(s.m_x, ch + 1)
                turn_tiles(turn[0], lambda t: xT[:, t * P:(t + 1) * P]).then_inc(s.e_turned, 1)
                pe.wait_ge(s.e_ready, 2 * NCH + 2 * ch + 1)
                turn_tiles(turn[1], lambda t: ln_h[:, t, :]).then_inc(s.e_back, 1)
                pe.wait_ge(s.e_out, NCH + ch + 1)
                for t in range(T):
                    last = mm(acc[:, t * M_HEADS:(t + 1) * M_HEADS], xnT[:, t * P:(t + 1) * P], m_win[:, M_DT:M_DT + M_HEADS])
                last.then_inc(s.m_dtf, 1)
                for bank, lo, n in ((proj[0], M_X, P), (proj[1], M_X + P, P), (sc[0], M_B, M_STATE), (sc[1], M_C, M_STATE)):
                    mm(bank[0:n, :], m_win[:, lo:lo + n], xnT[:]).then_inc(s.m_proj, 1)
                for i in range(2):
                    pe.wait_ge(s.m_cin_st, ch * 4 + i + 1)
                    for u in range(2):
                        t = 2 * i + u
                        last = mm(proj[i][:, u * M_INNER:(u + 1) * M_INNER], xnT[:, t * P:(t + 1) * P], m_win[:, M_Z:M_Z + M_INNER])
                    last.then_inc(s.m_zfull, 1)
                pe.wait_ge(s.m_a_st, ch + 1)
                U, ONE = upper[:, 0:P], upper[:, 2 * P:3 * P]
                for t in range(T):
                    av = [m_a[:, u * M_HEADS:(u + 1) * M_HEADS] for u in range(T)]
                    o = acc[:, 64 + t * M_HEADS:64 + (t + 1) * M_HEADS]
                    if t % 2:
                        mm(o, ONE, av[t - 1], stop=False)
                    last = mm(o, U, av[t], start=(t % 2 == 0))
                last.then_inc(s.m_cumf, 1)
                def segments(n):
                    b, h = n // M_HEADS, n % M_HEADS
                    pe.wait_ge(s.m_am_st, ch * 24 + 3 * (n + 1))
                    if n >= 2:
                        pe.wait_ge(s.m_L_st, ch * 8 + n - 1)
                    am = [m_am[:, (2 * b + u) * M_HEADS + h, :] for u in range(2)]
                    o = turn[n % 2]
                    mm(o[:, 0:P], am[0], U)
                    mm(o[:, P:2 * P], am[1], U)
                    mm(o[:, 2 * P:3 * P], am[0], ONE, stop=False)
                    mm(o[:, 2 * P:3 * P], m_ab[:, b * M_HEADS + h, :], U, start=False).then_inc(s.m_df, 1)
                for n in range(B * M_HEADS):
                    if n < 2:
                        segments(n)
                pe.wait_ge(s.m_cin_st, ch * 4 + 4)
                for i in range(2):
                    if i == 0:
                        pe.wait_ge(s.m_xc_st, ch * 4 + 2)
                    for u in range(2):
                        for j in range(2):
                            t = 2 * i + u
                            last = pe.transpose(sc[i][:, (2 * u + j) * P:(2 * u + j + 1) * P], m_xc[:, j, t * P:(t + 1) * P], ident[:])
                    last.then_inc(s.m_xf, 1)
                pe.wait_ge(s.m_xc_st, ch * 4 + 4)
                pe.wait_ge(s.m_z_st, ch * 2 + 2)
                for b in range(B):
                    for i, (ku, qu) in enumerate(((0, 0), (1, 1), (0, 1))):
                        last = mm(proj[b][:, i * P:(i + 1) * P], m_xc[0:M_STATE, 2, (2 * b + ku) * P:(2 * b + ku + 1) * P],
                                  m_xc[0:M_STATE, 3, (2 * b + qu) * P:(2 * b + qu + 1) * P])
                    last.then_inc(s.m_cbf, 1)
                for b in range(B):
                    pe.wait_ge(s.m_xdt_st, ch * 2 + b + 1)
                    for u in range(2):
                        last = mm(sc[b][:, u * M_INNER:(u + 1) * M_INNER], m_xc[0:M_STATE, 3, (2 * b + u) * P:(2 * b + u + 1) * P],
                                  m_init[:].rearrange("n h d -> n (h d)"))
                    last.then_inc(s.m_offf, 1)
                pe.wait_ge(s.m_ecum_st, ch + 1)
                for n in range(B * M_HEADS):
                    if n + 2 < B * M_HEADS:
                        segments(n + 2)
                    b, h = n // M_HEADS, n % M_HEADS
                    pe.wait_ge(s.m_M_st, ch * 8 + n + 1)
                    y = (ops, acc)[b]
                    M = m_M[n % 2]
                    xh = [m_xdt[:, 2 * b + u, h * HD:(h + 1) * HD] for u in range(2)]
                    mm(y[:, h * HD:(h + 1) * HD], M[:, 0:P], xh[0])
                    mm(y[:, M_INNER + h * HD:M_INNER + (h + 1) * HD], M[:, 2 * P:3 * P], xh[0], stop=False)
                    mm(y[:, M_INNER + h * HD:M_INNER + (h + 1) * HD], M[:, P:2 * P], xh[1], start=False).then_inc(s.m_yf, 1)
                pe.wait_ge(s.m_L_st, ch * 8 + B * M_HEADS)
                pe.wait_ge(s.m_yn, ch * 4 + T)
                for j in range(2):
                    for t in range(T):
                        last = pe.transpose(turn[j][:, t * P:(t + 1) * P], m_y[:, t, j * P:(j + 1) * P], ident[:])
                    last.then_inc(s.m_yt, 1)
                for j in range(2):
                    pe.wait_ge(s.m_yT_st, ch * 2 + j + 1)
                    last = mm(acc[:], m_wout[:, j, :], m_yT[:, j, :], start=(j == 0), stop=(j == 1))
                last.then_inc(s.m_acc, 1)
                finish(NCH + ch + 1)

            layers(ld)

            with pe.Fori(0, NCH) as ch:
                pe.wait_ge(s.fin_x, ch + 1)
                turn_tiles(turn[0], lambda t: xT[:, t * P:(t + 1) * P]).then_inc(s.fin_t, 1)
                pe.wait_ge(s.fin_st, ch + 1)


def _rotary(np, window, n, head):
    f = np.float32
    half = np.arange(0, head, 2, dtype=f)
    freq = np.arange(n, dtype=f)[:, None] * (f(1.0) / f(10000.0) ** (half / f(head)))[None, :]
    freq = np.concatenate([freq, freq], -1)
    base = (half + f(0.4 * head)) / f(1.4 * head)
    scale = base[None, :] ** ((np.arange(n, dtype=f) - n // 2) / f(window // 2))[:, None]
    scale = np.concatenate([scale, scale], -1)
    sign = np.concatenate([-np.ones(head // 2, f), np.ones(head // 2, f)])[None, :]
    cos, sin = np.cos(freq), np.sin(freq) * sign
    t = np.concatenate([cos * scale * f(8.0), sin * scale * f(8.0), cos / scale, sin / scale], -1).astype(f)
    return np.ascontiguousarray(t.reshape(n // 128, 128, 4 * head).transpose(1, 0, 2))


def _masks(np, window):
    i = (np.arange(128) % 64)[:, None]
    j = np.arange(window + 64)[None, :] - window
    band = (j > i) | (j < i - window)
    first = band | ((j < 0) & (np.arange(128)[:, None] < 64))
    return np.ascontiguousarray(np.stack([np.where(first, -1e30, 0.0), np.where(band, -1e30, 0.0)], 1).astype(np.float32))


def kernel(**inputs):
    import numpy as np
    import concourse.bacc as bacc
    from concourse.bass_utils import run_bass_kernel_spmd as run

    f = np.float32
    arr = {}

    def put(name, x):
        arr[name] = np.ascontiguousarray(x)

    put("x", inputs["L0_attn_x"])
    for n in ("Wq", "Wl", "Wk", "Wv", "Wo", "bv"):
        put("L0_attn_" + n, inputs["L0_attn_" + n])
    cols = np.zeros((128, 4), f)
    for i, n in enumerate(("bq", "bk", "bo")):
        cols[:, i] = inputs["L0_attn_" + n]
    cols[0:32, 3] = inputs["L0_attn_bl"]
    put("a_cols", cols)

    idx = np.arange(128)
    tri = (idx[:, None] <= idx[None, :]).astype(f)
    put("c_ident", np.eye(128, dtype=f))
    put("c_upper", np.concatenate([tri, tri, np.ones((128, 128), f)], 1))
    put("c_strict", (idx[:, None] > idx[None, :]).astype(f))
    put("c_headmask", ((idx[:, None] // 8 == np.arange(16)[None, :]) * (8 ** -0.5)).astype(f))

    for tag, pre, ins, names, window, heads in (
            ("lb", "L0f_", "L0_ffn_", ("Wqkv", "Wo", "W1", "W2"), 32, 16),
            ("ld", "L1f_", "L1_ffn_", ("wqkv", "wo", "w1", "w2"), 64, 8)):
        for n, m in zip(("wqkv", "wo", "w1", "w2"), names):
            put(pre + n, inputs[ins + m])
        g = np.asarray(inputs[ins + "ln_g"])
        layers = g.shape[0]
        v = np.zeros((layers, 128, 9), f)
        v[:, :, 0] = g
        v[:, :, 1] = inputs[ins + "ln_b"]
        v[:, :, 2] = inputs[ins + "b2"]
        b1 = np.asarray(inputs[ins + "b1"])
        for half in range(2):
            for i in range(3):
                n = min(128, 341 - 128 * i)
                lo = 341 * half + 128 * i
                v[:, 0:n, 3 + 3 * half + i] = b1[:, lo:lo + n]
        put(tag + "_vec", v)
        qs, ks = np.asarray(inputs[ins + "q_scale"]), np.asarray(inputs[ins + "k_scale"])
        swap = np.concatenate([np.arange(32, 64), np.arange(32)])
        put(tag + "_rows", np.concatenate([qs, qs[:, swap], ks, ks[:, swap]], 1))
        put(tag + "_rot", _rotary(np, window, 256, 64))
        put(tag + "_mask", _masks(np, window))

    put("m_win", np.asarray(inputs["L1_attn_in_proj_w"]).T)
    put("m_wout", np.asarray(inputs["L1_attn_out_proj_w"]).T)
    cw = np.zeros((128, 4, 5), f)
    w, bias = np.asarray(inputs["L1_attn_conv_w"]), np.asarray(inputs["L1_attn_conv_b"])
    for j, (lo, n) in enumerate(((0, 128), (128, 128), (256, 64), (320, 64))):
        cw[0:n, j, 0:4] = w[lo:lo + n]
        cw[0:n, j, 4] = bias[lo:lo + n]
    put("m_cw", cw)
    put("m_nw", np.asarray(inputs["L1_attn_norm_w"]).reshape(2, 128).T)
    put("m_init", np.asarray(inputs["L1_attn_init_states"]).transpose(2, 0, 1))
    put("m_rows", np.stack([np.asarray(inputs["L1_attn_" + n]) for n in ("dt_bias", "A_log", "D")]))

    nc = bacc.Bacc("TRN2", target_bir_lowering=False, num_devices=1)
    aps = {n: nc.dram_tensor("in_" + n, x.shape, mybir.dt.from_np(x.dtype), kind="ExternalInput").ap() for n, x in arr.items()}
    out = nc.dram_tensor("out_0", (16, 256, 128), F32, kind="ExternalOutput").ap()
    build(nc, aps, out)
    r = run(nc, [{"in_" + n: x for n, x in arr.items()}], core_ids=[0])
    return r.results[0]["out_0"]
```
